# Optimizing a Trainium2 kernel written in Bass

```python
import numpy as np
import jax
import jax.numpy as jnp

def _softmax(x, axis=-1):
    return jax.nn.softmax(x, axis=axis)

def _gelu(x):
    return jax.nn.gelu(x, approximate=True)

def _silu(x):
    return jax.nn.silu(x)

def _sigmoid(x):
    return jax.nn.sigmoid(x)

def _layernorm(x, axis=-1, eps=1e-05):
    m = jnp.mean(x, axis=axis, keepdims=True)
    v = jnp.var(x, axis=axis, keepdims=True)
    return (x - m) / jnp.sqrt(v + eps)

def _scatter_add(tgt, idx, src, axis=0):
    return tgt.at[idx].add(src)

def _segment_sum(src, seg, n):
    return jax.ops.segment_sum(src, seg, n)
kernel_name = 'mk_cond_seq_d1_seqx_r4_319652'

def setup_inputs(seed: int=0):
    np.random.seed(seed)
    _w = jnp.asarray

    def _rec_inputs():
        import jax
        import jax.numpy as jnp
        _rk = jax.random.key(seed)
        x = -0.0002928 + 1 * jax.random.normal(jax.random.fold_in(_rk, 1), (2, 1024, 256), jnp.float32)
        _lenS = 1024 - jax.random.randint(jax.random.fold_in(_rk, 7), (2,), 0, max(1, 1024 // 4) + 1, jnp.int32)
        _lenS2 = 1024 - jax.random.randint(jax.random.fold_in(_rk, 8), (2,), 0, max(1, 1024 // 4) + 1, jnp.int32)
        cond_1024 = 0.000887014 + 1.03683 * jax.random.normal(jax.random.fold_in(_rk, 11), (2, 256), jnp.float32)
        return (x, cond_1024)
    x, cond_1024 = _rec_inputs()

    def _L0_cond_setup():
        import math
        import jax, jax.numpy as jnp
        import numpy as np
        D_MODEL = 256
        N_HEADS = 16
        FFN_DIM = 1024
        EPS = 1e-05

        def _layernorm(x, w, b):
            mu = jnp.mean(x, axis=-1, keepdims=True)
            var = jnp.var(x, axis=-1, keepdims=True)
            return (x - mu) * jax.lax.rsqrt(var + EPS) * w + b

        def _modulate(x, shift, scale):
            return x * (1.0 + scale[:, None, :]) + shift[:, None, :]
        key = jax.random.key(seed)
        ks = jax.random.split(key, 16)
        B, S, D, F = (2, 512, D_MODEL, FFN_DIM)
        s = 0.02
        return {'x': jax.random.normal(ks[0], (B, S, D), jnp.float32), 't_emb': jax.random.normal(ks[1], (B, D), jnp.float32), 'ln1_w': jnp.ones((D,), jnp.float32), 'ln1_b': jnp.zeros((D,), jnp.float32), 'ln2_w': jnp.ones((D,), jnp.float32), 'ln2_b': jnp.zeros((D,), jnp.float32), 'wq': jax.random.normal(ks[2], (D, D), jnp.float32) * s, 'bq': jnp.zeros((D,), jnp.float32), 'wk': jax.random.normal(ks[3], (D, D), jnp.float32) * s, 'bk': jnp.zeros((D,), jnp.float32), 'wv': jax.random.normal(ks[4], (D, D), jnp.float32) * s, 'bv': jnp.zeros((D,), jnp.float32), 'wo': jax.random.normal(ks[5], (D, D), jnp.float32) * s, 'bo': jnp.zeros((D,), jnp.float32), 'wt_attn': jax.random.normal(ks[6], (D, 2 * D), jnp.float32) * s, 'bt_attn': jnp.zeros((2 * D,), jnp.float32), 'wt_ffn': jax.random.normal(ks[7], (D, 2 * D), jnp.float32) * s, 'bt_ffn': jnp.zeros((2 * D,), jnp.float32), 'w1': jax.random.normal(ks[8], (D, F), jnp.float32) * s, 'b1': jnp.zeros((F,), jnp.float32), 'w2': jax.random.normal(ks[9], (F, D), jnp.float32) * s, 'b2': jnp.zeros((D,), jnp.float32)}
    _L0_cond_all = _L0_cond_setup()
    _L0_cond_in = {k: v for k, v in _L0_cond_all.items() if k in ('ln1_w', 'ln1_b', 'ln2_w', 'ln2_b', 'wq', 'bq', 'wk', 'bk', 'wv', 'bv', 'wo', 'bo', 'wt_attn', 'bt_attn', 'wt_ffn', 'bt_ffn', 'w1', 'b1', 'w2', 'b2')}
    del _L0_cond_all
    return {'x': x, 'cond_1024': cond_1024, 'L0_cond_ln1_w': _L0_cond_in['ln1_w'], 'L0_cond_ln1_b': _L0_cond_in['ln1_b'], 'L0_cond_ln2_w': _L0_cond_in['ln2_w'], 'L0_cond_ln2_b': _L0_cond_in['ln2_b'], 'L0_cond_wq': _L0_cond_in['wq'], 'L0_cond_bq': _L0_cond_in['bq'], 'L0_cond_wk': _L0_cond_in['wk'], 'L0_cond_bk': _L0_cond_in['bk'], 'L0_cond_wv': _L0_cond_in['wv'], 'L0_cond_bv': _L0_cond_in['bv'], 'L0_cond_wo': _L0_cond_in['wo'], 'L0_cond_bo': _L0_cond_in['bo'], 'L0_cond_wt_attn': _L0_cond_in['wt_attn'], 'L0_cond_bt_attn': _L0_cond_in['bt_attn'], 'L0_cond_wt_ffn': _L0_cond_in['wt_ffn'], 'L0_cond_bt_ffn': _L0_cond_in['bt_ffn'], 'L0_cond_w1': _L0_cond_in['w1'], 'L0_cond_b1': _L0_cond_in['b1'], 'L0_cond_w2': _L0_cond_in['w2'], 'L0_cond_b2': _L0_cond_in['b2']}

def reference(x, cond_1024, L0_cond_ln1_w, L0_cond_ln1_b, L0_cond_ln2_w, L0_cond_ln2_b, L0_cond_wq, L0_cond_bq, L0_cond_wk, L0_cond_bk, L0_cond_wv, L0_cond_bv, L0_cond_wo, L0_cond_bo, L0_cond_wt_attn, L0_cond_bt_attn, L0_cond_wt_ffn, L0_cond_bt_ffn, L0_cond_w1, L0_cond_b1, L0_cond_w2, L0_cond_b2):
    import jax
    import jax.numpy as jnp

    def _L0_cond_ref(x, t_emb, ln1_w, ln1_b, ln2_w, ln2_b, wq, bq, wk, bk, wv, bv, wo, bo, wt_attn, bt_attn, wt_ffn, bt_ffn, w1, b1, w2, b2):
        import math
        import jax, jax.numpy as jnp
        import numpy as np
        D_MODEL = 256
        N_HEADS = 16
        FFN_DIM = 1024
        EPS = 1e-05

        def _layernorm(x, w, b):
            mu = jnp.mean(x, axis=-1, keepdims=True)
            var = jnp.var(x, axis=-1, keepdims=True)
            return (x - mu) * jax.lax.rsqrt(var + EPS) * w + b

        def _modulate(x, shift, scale):
            return x * (1.0 + scale[:, None, :]) + shift[:, None, :]
        B, S, D = x.shape
        H = N_HEADS
        hd = D // H
        residual = x
        xn = _layernorm(x, ln1_w, ln1_b)
        t_attn = t_emb @ wt_attn + bt_attn
        shift_a, scale_a = jnp.split(t_attn, 2, axis=-1)
        xn = _modulate(xn, shift_a, scale_a)
        q = (xn @ wq + bq).reshape(B, S, H, hd).transpose(0, 2, 1, 3)
        k = (xn @ wk + bk).reshape(B, S, H, hd).transpose(0, 2, 1, 3)
        v = (xn @ wv + bv).reshape(B, S, H, hd).transpose(0, 2, 1, 3)
        scores = jnp.einsum('bhqd,bhkd->bhqk', q, k) / math.sqrt(hd)
        attn = jax.nn.softmax(scores, axis=-1)
        out = jnp.einsum('bhqk,bhkd->bhqd', attn, v)
        out = out.transpose(0, 2, 1, 3).reshape(B, S, D)
        x = residual + (out @ wo + bo)
        residual = x
        xn = _layernorm(x, ln2_w, ln2_b)
        t_ffn = t_emb @ wt_ffn + bt_ffn
        shift_f, scale_f = jnp.split(t_ffn, 2, axis=-1)
        xn = _modulate(xn, shift_f, scale_f)
        h = jax.nn.gelu(xn @ w1 + b1, approximate=False)
        x = residual + (h @ w2 + b2)
        return x
    x = _L0_cond_ref(x, cond_1024, L0_cond_ln1_w, L0_cond_ln1_b, L0_cond_ln2_w, L0_cond_ln2_b, L0_cond_wq, L0_cond_bq, L0_cond_wk, L0_cond_bk, L0_cond_wv, L0_cond_bv, L0_cond_wo, L0_cond_bo, L0_cond_wt_attn, L0_cond_bt_attn, L0_cond_wt_ffn, L0_cond_bt_ffn, L0_cond_w1, L0_cond_b1, L0_cond_w2, L0_cond_b2)
    return x

_drawn_inputs = setup_inputs


def setup_inputs(seed=0):
    import zlib

    import numpy as np

    out = dict(_drawn_inputs(seed))
    spreads = {'L0_cond_ln1_w': (1.0, 0.6),
     'L0_cond_ln1_b': (0.0, 0.726),
     'L0_cond_ln2_w': (1.0, 0.6),
     'L0_cond_ln2_b': (0.0, 0.73),
     'L0_cond_bq': (0.0, 0.8),
     'L0_cond_bk': (0.0, 0.8),
     'L0_cond_bv': (0.0, 0.271),
     'L0_cond_bo': (0.0, 0.1),
     'L0_cond_bt_attn': (0.0, 0.748),
     'L0_cond_bt_ffn': (0.0, 0.482),
     'L0_cond_b1': (0.0, 0.1),
     'L0_cond_b2': (0.0, 0.1)}
    factors = {'L0_cond_wq': 8.0, 'L0_cond_wk': 8.0}
    for name, (base, spread) in spreads.items():
        noise = np.random.default_rng([zlib.crc32(name.encode()), seed]).standard_normal(out[name].shape)
        drawn = base * np.exp(spread * noise) if base else spread * noise
        out[name] = jnp.asarray(drawn.astype(out[name].dtype))
    for name, factor in factors.items():
        out[name] = (out[name] * factor).astype(out[name].dtype)
    return out
```

```python
from contextlib import ExitStack

import concourse.bass as bass
from concourse import mybir

F32 = mybir.dt.float32
BF16 = mybir.dt.bfloat16
ACT = mybir.ActivationFunctionType
ALU = mybir.AluOpType
AX_X = mybir.AxisListType.X

P = 128
EPS = 1e-5
TERMS = [(0, 0), (0, 1), (1, 0), (0, 2), (2, 0), (1, 1)]

LN_W, LN_B, BQ, BK, BT, B1, COND = (0, 4), (2, 6), 8, 10, 12, 20, 28


def layer_program(nc, x, cond, ln1_w, ln1_b, ln2_w, ln2_b, wq, bq, wk, bk, wv, bv, wo, bo,
                  wt_attn, bt_attn, wt_ffn, bt_ffn, w1, b1, w2, b2, out):
    B, S, D = x.shape
    F = w1.shape[1]
    H = 16
    HD = D // H
    DC = D // P
    FC = F // P
    NT = B * S // P
    TB = S // P
    HG = 4
    NG = B * H // HG
    VW = HD + 1
    NTERM = len(TERMS)
    KS = NTERM * HD
    SLOTS = 3
    HS = S // 512
    STEPS = HS * TB
    TG = B * S // 512
    SCALE = float(HD) ** -0.5
    assert (D, F, S, B, HD) == (256, 1024, 1024, 2, 16)

    x_tiles = x.rearrange("b (t p) d -> p (b t) d", p=P)
    out_tiles = out.rearrange("b (t p) d -> p (b t) d", p=P)

    with ExitStack() as ctx:
        def sb(name, shape, dt):
            return ctx.enter_context(nc.sbuf_tensor(name, shape, dt))

        def sem(name):
            return ctx.enter_context(nc.semaphore(name))

        x_sb = sb("x_sb", [P, NT, D], F32)
        work = sb("work", [P, 4096], F32)
        attn_sb = sb("attn_sb", [P, NG // 2, TB, 2, HG * HD], F32)
        parts = sb("parts", [P, 2 * 3, B * DC * S], BF16)
        stack = sb("stack", [P, SLOTS * HG * 2, S], BF16)
        v_all = sb("v_all", [P, NG, TB, HG * VW], F32)
        v_group = sb("v_group", [P, TB, HG, 32], F32)
        wq_sb = sb("wq_sb", [P, DC, D], F32)
        wk_sb = sb("wk_sb", [P, DC, D], F32)
        wv_sb = sb("wv_sb", [P, DC, D], F32)
        wo_sb = sb("wo_sb", [P, DC, D], F32)
        wt_sb = sb("wt_sb", [P, 2, DC, 2 * D], F32)
        w1_sb = sb("w1_sb", [P, DC, F], F32)
        w2_sb = sb("w2_sb", [P, FC, D], F32)
        rows = sb("rows", [32, P], F32)
        cols = sb("cols", [P, 32], F32)
        bv_all = sb("bv_all", [P, D], F32)
        bo_all = sb("bo_all", [P, D], F32)
        b2_all = sb("b2_all", [P, D], F32)
        ident = sb("ident", [P, P], F32)
        ident_bf = sb("ident_bf", [P, P], BF16)
        t_mod = sb("t_mod", [P, 8, B], F32)
        mod_one = sb("mod_one", [P, 2, DC, B], F32)
        mod_mul = sb("mod_mul", [P, 2, DC, B], F32)
        mod_add = sb("mod_add", [P, 2, DC, B], F32)
        bn = sb("bn", [P, NT, 6], F32)
        mean_var = sb("mean_var", [P, NT, 2], F32)
        eps_col = sb("eps_col", [P, 1], F32)
        std = sb("std", [P, NT], F32)
        rstd = sb("rstd", [P, NT], F32)
        rest = sb("rest", [P, 2, 512], F32)
        row_max = sb("row_max", [P, 2, TB], F32)
        neg_max = sb("neg_max", [P, 2, 2, TB], BF16)
        neg_max_t = sb("neg_max_t", [16, HG, P], BF16)
        rsum = sb("rsum", [P, 4 * HG], F32)

        out_t = rest[:, 0, :]
        xn_t = work[:, :].rearrange("p (c t) -> p c t", c=DC)
        probs = work[:, :].rearrange("p (a j q) -> p a j q", a=2, j=HG)
        xhat = attn_sb[:, :, :, :, :].rearrange("p n t o f -> p (n t o f)").rearrange("p (t d) -> p t d", d=D)
        attn_out = attn_sb[:, :, :, :, :]
        parts_f32 = parts[:, :, :].rearrange("p a t -> p (a t)").bitcast(F32)
        hid_t = parts_f32[:, 0:FC * 512].rearrange("p (f t) -> p f t", f=FC)
        attn_t = parts_f32[:, FC * 512:(FC + 4) * 512].rearrange("p (a c t) -> p a c t", a=2, c=DC)
        xhat2 = parts_f32[:, (FC + 4) * 512:(FC + 8) * 512].rearrange("p (a t d) -> p a t d", a=2, t=4)
        xn2_t = parts_f32[:, (FC + 8) * 512:(FC + 16) * 512].rearrange("p (c t) -> p c t", c=DC)

        psum = ctx.enter_context(nc.psum_tensor("psum", [P, 8, 512], F32))
        ST_BANK, PV_BANK, MISC_BANK = 4, 6, 7

        rows_in, cond_in, wt_in = sem("rows_in"), sem("cond_in"), sem("wt_in")
        x_in = [sem(f"x_in{b}") for b in range(B)]
        wqk_in, wv_in, late_in = sem("wqk_in"), sem("wv_in"), sem("late_in")
        ident_made, ones_made, v_ones_made = sem("ident_made"), sem("ones_made"), sem("v_ones_made")
        cols_psum, cols_ready = sem("cols_psum"), sem("cols_ready")
        mod_psum, mod_step = sem("mod_psum"), sem("mod_step")
        stats_step, var_ready, std_ready, rstd_ready = (
            sem("stats_step"), sem("var_ready"), sem("std_ready"), sem("rstd_ready"))
        xhat_ready, xn_ready = sem("xhat_ready"), sem("xn_ready")
        a_psum = sem("a_psum")
        high_ready, rest_ready, mid_ready, parts_ready = (
            sem("high_ready"), sem("rest_ready"), sem("mid_ready"), sem("parts_ready"))
        v_ready = sem("v_ready")
        stack_in = [sem(f"stack_in{j}") for j in range(HG)]
        smax_psum, smax_read, neg_ready = sem("smax_psum"), sem("smax_read"), sem("neg_ready")
        row_max_done, neg_high = sem("row_max_done"), sem("neg_high")
        misc_psum = sem("misc_psum")
        neg_t_ready = sem("neg_t_ready")
        max_row_in = [sem(f"max_row_in{j}") for j in range(HG)]
        st_psum, probs_ready = sem("st_psum"), sem("probs_ready")
        pv_step = sem("pv_step")
        v_group_ready, out_t_ready = sem("v_group_ready"), sem("out_t_ready")
        rsum_ready, attn_ready = sem("rsum_ready"), sem("attn_ready")
        bo_added, b2_added = sem("bo_added"), sem("b2_added")
        c_psum = sem("c_psum")
        attn_t_ready, x1_ready = sem("attn_t_ready"), sem("x1_ready")
        stats2_step, var2_ready, std2_ready, rstd2_ready = (
            sem("stats2_step"), sem("var2_ready"), sem("std2_ready"), sem("rstd2_ready"))
        xhat2_ready, xn2_ready = sem("xhat2_ready"), sem("xn2_ready")
        hid_psum, hid_ready = sem("hid_psum"), sem("hid_ready")
        out_psum, out_ready, out_stored = sem("out_psum"), sem("out_ready"), sem("out_stored")

        a_jobs = []
        for b in range(B):
            tgs = range(b * TG // B, (b + 1) * TG // B)
            a_jobs += [("T", b, tg, c) for tg in tgs for c in range(DC)]
            for c in range(DC):
                a_jobs += [(kind, b, tg, c) for tg in tgs for kind in "QK"]
            a_jobs += [("V", b, tg, pair) for tg in tgs for pair in range(2)]
        A_RING = 3

        def early_tiles(i):
            n = i - len(a_jobs) // B
            return range(2 * n - 2, 2 * n) if n >= 1 else range(0)

        a_index = {job: i for i, job in enumerate(a_jobs)}
        qk_jobs = [job for job in a_jobs if job[0] in "QK"]

        DEV2_STEP = 9

        def jobs(*names):
            return [(name[0], int(name[1]), c) for name in names for c in range(2)]

        c_early = jobs("A0", "A1", "O0", "O1") + [None, None, None] + jobs("T0", "T1")
        c_middle, c_late = jobs("A2", "A3", "O2", "O3"), jobs("T2", "T3")
        c_index = {job: i for i, job in enumerate([x for x in c_early if x] + c_middle + c_late)}

        def c_bank(kind, tg, c):
            if tg < 2:
                return c
            return {"A": 2 * (tg % 2), "O": 4, "T": 6}[kind] + c

        LAST_MAX_STEP = (NG - 1) * STEPS - 4

        def st_bank(tile):
            return (4, 5, 2, 3)[tile % HG] if tile // HG > LAST_MAX_STEP else ST_BANK + tile % 2

        def a_read(i):
            kind, b, tg, c = a_jobs[i]
            if kind == "T":
                return xn_ready, DC * tg + c + 1
            if kind == "V":
                return v_ready, 2 * (2 * tg + c + 1)
            return rest_ready, qk_jobs.index(a_jobs[i]) + 1

        def c_read(kind, tg, c):
            return {"A": attn_t_ready, "O": x1_ready, "T": xn2_ready}[kind], 2 * tg + c + 1

        c_order = [x for x in c_early if x] + c_middle + c_late

        def c_before(job):
            return [x for x in c_order[:c_order.index(job)] if c_bank(*x) == c_bank(*job)][-1:]

        def token_slice(b, c, tg):
            at = (b * DC + c) * S + (tg % (TG // B)) * 512
            return slice(at, at + 512)

        def head_in_stack(slot, j, side, first, size):
            return bass.ds(slot + ((2 * j + side) * S + first), size)

        def slot_of(group):
            return (group % SLOTS) * (HG * 2 * S)

        def misc_use(group, j):
            return j + 1 if group == 0 else HG + 6 * (group - 1) + j + 1 + (j >= 2)

        stack_flat = stack[:, :, :].rearrange("p a t -> p (a t)")
        parts_flat = parts[:, :, :]

        block = ctx.enter_context(nc.Block())

        @block.sync
        def _(sp):
            for at, vec in ((0, ln1_w), (2, ln1_b), (4, ln2_w), (6, ln2_b), (8, bq), (10, bk),
                            (12, bt_attn), (16, bt_ffn), (20, b1)):
                r = vec.rearrange("(r k) -> r k", k=P)
                sp.dma_start(rows[at:at + r.shape[0], :], r).then_inc(rows_in, 16)
            sp.dma_start(rows[28:32, :], cond.rearrange("b (c k) -> (b c) k", k=P)).then_inc(rows_in, 16)
            sp.dma_start(x_sb[:, TB:2 * TB, :], x_tiles[:, TB:2 * TB, :]).then_inc(x_in[1], 16)
            sp.dma_start(wv_sb[:, :, :], wv.rearrange("(c k) n -> k c n", k=P)).then_inc(wv_in, 16)
            sp.dma_start(bv_all[:, :], bv.partition_broadcast(P)).then_inc(wv_in, 16)
            for dst, src in ((wo_sb, wo), (w1_sb, w1), (w2_sb, w2)):
                sp.dma_start(dst[:, :, :], src.rearrange("(c k) n -> k c n", k=P)).then_inc(late_in, 16)
            for dst, src in ((bo_all, bo), (b2_all, b2)):
                sp.dma_start(dst[:, :], src.partition_broadcast(P)).then_inc(late_in, 16)

            def load_head(group, pair, odd, j):
                p0 = 64 * odd + 16 * j
                slot = (group % SLOTS) * (HG * 2)
                for t, (a, b) in enumerate(TERMS):
                    src = parts_flat[p0:p0 + HD, a:4 + b:3 + b - a, bass.ds(pair * S, S)]
                    at = slot + 2 * j
                    sp.dma_start(stack[t * HD:(t + 1) * HD, bass.ds(at, 2), :], src).then_inc(stack_in[j], 16)

            def store_max(group, j):
                slot = slot_of(group)
                sp.wait_ge(neg_t_ready, 4 * group + j + 1)
                for part in range(2):
                    sp.dma_start(stack_flat[KS + part:KS + part + 1, head_in_stack(slot, j, 0, 0, S)],
                                 neg_max_t[part * TB:(part + 1) * TB, j, :]).then_inc(max_row_in[j], 16)

            sp.wait_ge(parts_ready, 4)
            for j in range(HG):
                load_head(0, 0, 0, j)
            for j in range(HG):
                sp.wait_ge(stack_in[j], 16 * NTERM)
                load_head(1, 0, 1, j)
                store_max(0, j)
            sp.wait_ge(parts_ready, len(qk_jobs))
            for group in range(2, NG):
                sp.wait_ge(st_psum, (group - 2) * (STEPS * HG) + 1)
                for j in range(HG):
                    sp.wait_ge(stack_in[j], 16 * NTERM * group)
                    load_head(group, group // 2, group % 2, j)
                    store_max(group - 1, j)
            for j in range(HG):
                store_max(NG - 1, j)
            with sp.Fori(0, TG) as tg:
                for pair in range(2):
                    sp.wait_ge(out_ready, 2 + tg * 2 + (pair + 1))
                    sp.dma_start(out_tiles[:, bass.ds(tg * 4 + 2 * pair, 2), :],
                                 x_sb[:, bass.ds(tg * 4 + 2 * pair, 2), :]).then_inc(out_stored, 16)
            sp.wait_ge(out_stored, 16 * 2 * TG)

        @block.gpsimd
        def _(pool):
            nc.gpsimd.memset(ident[:, :], 0.0).then_inc(ident_made, 1)
            pool.wait_ge(ident_made, 1)
            nc.gpsimd.affine_select(out=ident[:, :], in_=ident[:, :], compare_op=ALU.not_equal, fill=1.0,
                                    base=0, pattern=[[-1, P]], channel_multiplier=1).then_inc(ident_made, 1)
            pool.wait_ge(ident_made, 2)
            nc.gpsimd.tensor_copy(ident_bf[:, :], ident[:, :]).then_inc(ident_made, 1)
            nc.gpsimd.memset(v_all[:, :, :, :], 1.0).then_inc(v_ones_made, 1)
            nc.gpsimd.memset(v_group[:, :, :, :], 0.0).then_inc(v_ones_made, 1)
            pool.wait_ge(v_ones_made, 2)
            for s in range(SLOTS):
                sides = stack[KS:P, s * HG * 2:(s + 1) * HG * 2, :]
                nc.gpsimd.memset(sides[:, 1::2, :], 1.0).then_inc(ones_made, 1)
            pool.wait_ge(ones_made, SLOTS)
            for i, (kind, b, tg, c) in enumerate(qk_jobs):
                side = 3 * (kind == "K")
                pool.wait_ge(mid_ready, i + 1)
                nc.gpsimd.tensor_tensor(parts[:, side + 2, token_slice(b, c, tg)], rest[:, i % 2, :],
                                        parts[:, side + 1, token_slice(b, c, tg)],
                                        ALU.subtract).then_inc(parts_ready, 1)

            def fill_v(group, half):
                nc.gpsimd.tensor_copy(
                    v_group[:, half * 4:half * 4 + 4, :, 0:VW],
                    v_all[:, bass.ds(group, 1), half * 4:half * 4 + 4, :].rearrange(
                        "p n k (j w) -> p (n k) j w", j=HG)).then_inc(v_group_ready, 1)

            pool.wait_ge(v_ready, 8)
            pool.wait_ge(v_ones_made, 2)
            for half in range(2):
                fill_v(0, half)
            pool.wait_ge(late_in, 16 * 5)
            for t in range(NT):
                nc.gpsimd.tensor_tensor(x_sb[:, t, :], x_sb[:, t, :], bo_all[:, :], ALU.add).then_inc(bo_added, 1)
            with pool.Fori(1, NG) as group:
                for half in range(2):
                    pool.wait_ge(pv_step, group * STEPS - (4 - 4 * half))
                    fill_v(group, half)
            for b in range(B):
                pool.wait_ge(xhat2_ready, (b + 1) * TB)
                for t in range(b * TB, (b + 1) * TB):
                    nc.gpsimd.tensor_tensor(x_sb[:, t, :], x_sb[:, t, :], b2_all[:, :],
                                            ALU.add).then_inc(b2_added, 1)

        @block.tensor
        def _(pe):
            pe.wait_ge(ident_made, 2)
            pe.wait_ge(rows_in, 16 * 10)
            nc.tensor.transpose(psum[:, 0, 0:32], rows[:, :], ident[0:32, 0:32]).then_inc(cols_psum, 1)
            pe.wait_ge(cols_ready, 1)
            pe.wait_ge(wt_in, 32)
            for which in range(2):
                for f in range(4):
                    for c in range(DC):
                        last = nc.tensor.matmul(psum[:, 1, (4 * which + f) * B:(4 * which + f + 1) * B],
                                                wt_sb[:, which, c, f * P:(f + 1) * P],
                                                cols[:, COND + c:COND + c + 3:2],
                                                start=(c == 0), stop=(c == DC - 1))
            last.then_inc(mod_psum, 1)

            def scores_for_max(tile, slot, j, qc, half):
                if half == 0 and tile >= 2:
                    pe.wait_ge(smax_read, tile - 1)
                last = nc.tensor.matmul(
                    psum[:, 2 * (qc % 2) + half, :],
                    stack_flat[0:KS, head_in_stack(slot, j, 0, qc * P, P)],
                    stack_flat[0:KS, head_in_stack(slot, j, 1, half * 512, 512)],
                    start=True, stop=True)
                if half == 1:
                    last.then_inc(smax_psum, 1)

            def turn_max(head, j):
                if head:
                    pe.wait_ge(neg_t_ready, head)
                pe.wait_ge(neg_ready, head + 1)
                nc.tensor.transpose(psum[0:16, MISC_BANK, 0:64].bitcast(BF16),
                                    neg_max[:, j % 2, :, :].rearrange("p a t -> p (a t)"),
                                    ident_bf[:, :]).then_inc(misc_psum, 1)

            def scores_for_exp(slot, step, j, tile):
                half, kc = divmod(step, TB)
                same = [u for u in range(max(tile - HG, 0), tile) if st_bank(u) == st_bank(tile)]
                if same:
                    pe.wait_ge(probs_ready, same[-1] + 1)
                elif tile > HG:
                    pe.wait_ge(smax_read, NG * HG * TB)
                last = nc.tensor.matmul(
                    psum[:, st_bank(tile), :],
                    stack_flat[0:KS + 2, head_in_stack(slot, j, 1, kc * P, P)],
                    stack_flat[0:KS + 2, head_in_stack(slot, j, 0, half * 512, 512)],
                    start=True, stop=True)
                last.then_inc(st_psum, 1)
                return last

            def first_maxima(tile):
                head, qc = divmod(tile, TB)
                if qc == 0:
                    pe.wait_ge(stack_in[head % HG], 16 * NTERM * (head // HG + 1))
                for half in range(2):
                    scores_for_max(tile, slot_of(head // HG), head % HG, qc, half)
                if qc == 3 and head:
                    turn_max(head - 1, head - 1)

            pe.wait_ge(ident_made, 3)
            for i, (kind, b, tg, c) in enumerate(a_jobs):
                for tile in early_tiles(i):
                    first_maxima(tile)
                bank = 4 + i % A_RING
                if i >= A_RING:
                    pe.wait_ge(*a_read(i - A_RING))
                if kind == "T":
                    pe.wait_ge(xhat_ready, 4 * tg + 4)
                    for t in range(4):
                        last = nc.tensor.transpose(psum[:, bank, t * P:(t + 1) * P],
                                                   xhat[:, 4 * tg + t, c * P:(c + 1) * P], ident[:, :])
                    last.then_inc(a_psum, 1)
                    continue
                pe.wait_ge(xn_ready, DC * (tg + 1))
                if kind in "QK":
                    pe.wait_ge(wqk_in, 32)
                    w = wq_sb if kind == "Q" else wk_sb
                    for k in range(DC):
                        last = nc.tensor.matmul(psum[:, bank, :], w[:, k, c * P:(c + 1) * P],
                                                xn_t[:, k, tg * 512:(tg + 1) * 512],
                                                start=(k == 0), stop=(k == DC - 1))
                else:
                    pe.wait_ge(wv_in, 32)
                    for t in range(2):
                        token = (4 * tg + 2 * c + t) * P
                        for k in range(DC):
                            last = nc.tensor.matmul(psum[:, bank, t * D:(t + 1) * D],
                                                    xn_t[:, k, token:token + P], wv_sb[:, k, :],
                                                    start=(k == 0), stop=(k == DC - 1))
                last.then_inc(a_psum, 1)

            for tile in range(early_tiles(len(a_jobs) - 1).stop, (HG + 1) * TB):
                first_maxima(tile)
            for i in range(len(a_jobs) - A_RING, len(a_jobs)):
                pe.wait_ge(*a_read(i))
            pe.wait_ge(ones_made, SLOTS)
            for j in range(HG):
                pe.wait_ge(max_row_in[j], 32)
                scores_for_exp(0, 0, j, j)

            def c_job(kind, tg, c):
                bank = c_bank(kind, tg, c)
                for job in c_before((kind, tg, c)):
                    pe.wait_ge(*c_read(*job))
                if kind == "A":
                    for t in range(4):
                        b, tb = divmod(4 * tg + t, TB)
                        last = nc.tensor.transpose(
                            psum[:, bank, t * P:(t + 1) * P],
                            attn_out[:, b * DC + c, tb, :, :].rearrange("p o f -> p (o f)"), ident[:, :])
                elif kind == "O":
                    pe.wait_ge(attn_t_ready, DC * (tg + 1))
                    for t in range(2):
                        at = (2 * c + t) * P
                        for k in range(DC):
                            last = nc.tensor.matmul(psum[:, bank, t * D:(t + 1) * D],
                                                    attn_t[:, tg % 2, k, at:at + P], wo_sb[:, k, :],
                                                    start=(k == 0), stop=(k == DC - 1))
                else:
                    pe.wait_ge(xhat2_ready, 4 * (tg + 1))
                    for t in range(4):
                        last = nc.tensor.transpose(psum[:, bank, t * P:(t + 1) * P],
                                                   xhat2[:, tg % 2, t, c * P:(c + 1) * P], ident[:, :])
                last.then_inc(c_psum, 1)

            def mlp_turn(tg):
                for f in range(FC):
                    if f >= 4:
                        pe.wait_ge(hid_ready, tg * FC + (f - 3))
                    for k in range(DC):
                        last = nc.tensor.matmul(psum[:, f % 4, :], w1_sb[:, k, f * P:(f + 1) * P],
                                                xn2_t[:, k, bass.ds(tg * 512, 512)],
                                                start=(k == 0), stop=(k == DC - 1))
                    last.then_inc(hid_psum, 1)
                for pair in range(2):
                    pe.wait_ge(out_ready, tg * 2 + (pair + 1))
                    for t in range(2):
                        at = (2 * pair + t) * P
                        for f in range(FC):
                            if pair == 0 and t == 0:
                                pe.wait_ge(hid_ready, tg * FC + (f + 1))
                            last = nc.tensor.matmul(psum[:, 4 + pair, t * D:(t + 1) * D],
                                                    hid_t[:, f, at:at + P], w2_sb[:, f, :],
                                                    start=(f == 0), stop=(f == FC - 1))
                    last.then_inc(out_psum, 1)

            def group_steps(group):
                more = group + 1 < NG
                slot, next_slot = slot_of(group), slot_of(group + 1)
                for step in range(STEPS):
                    ahead = (group + 1) * HG + 1 + step // 4
                    ahead_group, ahead_j = divmod(ahead, HG)
                    qc = (2 * step) % TB
                    last_of_group = step + 1 == STEPS

                    def next_scores(j):
                        if last_of_group and not more:
                            return
                        if last_of_group:
                            pe.wait_ge(max_row_in[j], 32 * (group + 2))
                        scores_for_exp(next_slot if last_of_group else slot, (step + 1) % STEPS, j,
                                       (group * STEPS + step + 1) * HG + j)

                    def max_scores(tile, half):
                        if ahead < NG * HG:
                            scores_for_max(ahead * TB + qc + tile, slot_of(ahead_group), ahead_j, qc + tile, half)

                    if step % 4 == 0 and ahead < NG * HG:
                        pe.wait_ge(stack_in[ahead_j], 16 * NTERM * (ahead_group + 1))
                    max_scores(0, 0)
                    next_scores(0)
                    max_scores(0, 1)
                    next_scores(1)
                    pe.wait_ge(probs_ready, (group * STEPS + step + 1) * HG)
                    if step == 0 or step == 4:
                        pe.wait_ge(v_group_ready, group * 2 + 1 + step // 4)
                    if step % TB == 0 and (group or step):
                        pe.wait_ge(out_t_ready, group * 2 + step // TB)
                    for j in range(HG):
                        last = nc.tensor.matmul(psum[32 * j:32 * j + 32, PV_BANK, :],
                                                v_group[:, step % TB, j, :], probs[:, step % 2, j, :],
                                                start=(step % TB == 0), stop=(step % TB == TB - 1))
                    last.then_inc(pv_step, 1)
                    next_scores(2)
                    max_scores(1, 0)
                    next_scores(3)
                    max_scores(1, 1)
                    if step % 4 == 0 and more:
                        if step % TB == 0 and (group or step):
                            pe.wait_ge(attn_ready, group * 2 + step // TB)
                        turn_max((group + 1) * HG + step // 4, step // 4)
                    if step % TB == TB - 1:
                        half = step // TB
                        if more:
                            pe.wait_ge(neg_t_ready, (group + 1) * HG + 2 * half + 2)
                        else:
                            pe.wait_ge(attn_ready, group * 2 + half)
                        pe.wait_ge(out_t_ready, group * 2 + half + 1)
                        for t in range(4):
                            last = nc.tensor.transpose(psum[:, MISC_BANK, t * P:(t + 1) * P],
                                                       out_t[:, t * P:(t + 1) * P], ident[:, :])
                        last.then_inc(misc_psum, 1)
                    if not more and step < len(c_early) and c_early[step]:
                        if step == 0:
                            pe.wait_ge(smax_read, NG * HG * TB)
                            pe.wait_ge(attn_ready, NG)
                            pe.wait_ge(late_in, 16 * 5)
                        c_job(*c_early[step])

            for group in range(NG):
                group_steps(group)

            pe.wait_ge(attn_ready, 2 * NG)
            for job in c_middle:
                c_job(*job)
            pe.wait_ge(attn_t_ready, DC * TG)
            pe.wait_ge(x1_ready, 2 * TG)
            pe.wait_ge(xn2_ready, DC * 2)
            mlp_turn(0)
            for job in c_late:
                c_job(*job)
            pe.wait_ge(xn2_ready, DC * TG)
            with pe.Fori(1, TG) as tg:
                mlp_turn(tg)

        @block.scalar
        def _(act):
            act.dma_start(x_sb[:, 0:TB, :], x_tiles[:, 0:TB, :]).then_inc(x_in[0], 16)
            for which, w in enumerate((wt_attn, wt_ffn)):
                act.dma_start(wt_sb[:, which, :, :], w.rearrange("(c k) n -> k c n", k=P)).then_inc(wt_in, 16)
            for dst, src in ((wq_sb, wq), (wk_sb, wk)):
                act.dma_start(dst[:, :, :], src.rearrange("(c k) n -> k c n", k=P)).then_inc(wqk_in, 16)

            def deviation(b):
                act.wait_ge(var_ready, b + 1)
                nc.scalar.activation(std[:, b * TB:(b + 1) * TB], mean_var[:, b * TB:(b + 1) * TB, 1],
                                     ACT.Sqrt, bias=eps_col[:, 0:1]).then_inc(std_ready, 1)

            def xn_out(tg, c, b):
                i = a_index[("T", b, tg, c)]
                act.wait_ge(a_psum, i + 1)
                nc.scalar.activation(xn_t[:, c, tg * 512:(tg + 1) * 512], psum[:, 4 + i % A_RING, :], ACT.Identity,
                                     bias=mod_add[:, 0, c, b:b + 1],
                                     scale=mod_mul[:, 0, c, b:b + 1]).then_inc(xn_ready, 1)

            def high_part(i):
                kind, b, tg, c = qk_jobs[i]
                at = a_index[qk_jobs[i]]
                act.wait_ge(a_psum, at + 1)
                col = (BQ if kind == "Q" else BK) + c
                nc.scalar.activation(parts[:, 3 * (kind == "K"), token_slice(b, c, tg)], psum[:, 4 + at % A_RING, :],
                                     ACT.Identity, bias=cols[:, col:col + 1]).then_inc(high_ready, 1)

            def middle_part(i):
                kind, b, tg, c = qk_jobs[i]
                act.wait_ge(rest_ready, i + 1)
                nc.scalar.copy(parts[:, 3 * (kind == "K") + 1, token_slice(b, c, tg)],
                               rest[:, i % 2, :]).then_inc(mid_ready, 1)

            def turned_max(group, j):
                act.wait_ge(misc_psum, misc_use(group, j))
                if group:
                    act.wait_ge(max_row_in[j], 32 * group)
                nc.scalar.copy(neg_max_t[:, j, :], psum[0:16, MISC_BANK, 0:64].bitcast(BF16)).then_inc(neg_t_ready, 1)

            def first_turned(tile):
                if tile % TB == 3 and tile > TB:
                    turned_max(0, tile // TB - 1)

            deviation(0)
            act.wait_ge(mod_step, 8)
            for i, (kind, b, tg, c) in enumerate(a_jobs):
                for tile in early_tiles(i):
                    first_turned(tile)
                if kind == "T":
                    xn_out(tg, c, b)
                if kind in "QK":
                    n = qk_jobs.index(a_jobs[i])
                    high_part(n)
                    if n % (len(qk_jobs) // B):
                        middle_part(n - 1)
                    if n == 2:
                        deviation(1)
                if kind == "V" and tg % (TG // B) == 0 and c == 0:
                    middle_part((b + 1) * len(qk_jobs) // B - 1)
            for tile in range(early_tiles(len(a_jobs) - 1).stop, (HG + 1) * TB):
                first_turned(tile)

            def exponentials(tile):
                act.wait_ge(st_psum, tile + 1)
                nc.scalar.activation(probs[:, tile // HG % 2, tile % HG, :], psum[:, st_bank(tile), :], ACT.Exp,
                                     scale=SCALE).then_inc(probs_ready, 1)

            act.wait_ge(a_psum, len(a_jobs))
            def deviation2(b):
                act.wait_ge(var2_ready, 2 * b + 2)
                nc.scalar.activation(std[:, b * TB:(b + 1) * TB], mean_var[:, b * TB:(b + 1) * TB, 1],
                                     ACT.Sqrt, bias=eps_col[:, 0:1]).then_inc(std2_ready, 1)

            for j in range(HG):
                exponentials(j)
            for group in range(NG):
                more = group + 1 < NG
                for step in range(STEPS):
                    for j in range(HG):
                        if step + 1 < STEPS or more:
                            if j == 0 and (group or step):
                                act.wait_ge(pv_step, group * STEPS + step)
                            exponentials((group * STEPS + step + 1) * HG + j)
                        if j == 1 and step % 4 == 1 and more:
                            turned_max(group + 1, step // 4)
                        if j == 1 and step == DEV2_STEP and not more:
                            deviation2(0)
                        if step % TB == TB - 1 and j == 1:
                            half = step // TB
                            act.wait_ge(pv_step, group * STEPS + step + 1)
                            if group or half:
                                act.wait_ge(attn_ready, group * 2 + half)
                            nc.scalar.copy(out_t, psum[:, PV_BANK, :]).then_inc(out_t_ready, 1)

            def c_job(kind, tg, c):
                act.wait_ge(c_psum, c_index[kind, tg, c] + 1)
                src = psum[:, c_bank(kind, tg, c), :]
                if kind == "A":
                    nc.scalar.copy(attn_t[:, tg % 2, c, :], src).then_inc(attn_t_ready, 1)
                else:
                    b = tg * B // TG
                    nc.scalar.activation(xn2_t[:, c, tg * 512:(tg + 1) * 512], src, ACT.Identity,
                                         bias=mod_add[:, 1, c, b:b + 1],
                                         scale=mod_mul[:, 1, c, b:b + 1]).then_inc(xn2_ready, 1)

            def mlp_turn(tg):
                for f in range(FC):
                    act.wait_ge(hid_psum, tg * FC + (f + 1))
                    nc.scalar.activation(hid_t[:, f, :], psum[:, f % 4, :], ACT.Gelu,
                                         bias=cols[:, B1 + f:B1 + f + 1]).then_inc(hid_ready, 1)

            for job in c_middle[:4]:
                c_job(*job)
            mlp_turn(0)
            deviation2(1)
            for job in c_late:
                c_job(*job)
            with act.Fori(1, TG) as tg:
                mlp_turn(tg)

        @block.vector
        def _(dve):
            nc.vector.memset(eps_col[:, :], EPS).then_inc(stats_step, 1)
            nc.vector.memset(rsum[:, :], 0.0).then_inc(out_ready, 2)

            def stats(b):
                dve.wait_ge(x_in[b], 16)
                for t in range(b * TB, (b + 1) * TB):
                    nc.vector.bn_stats(bn[:, t, :], x_sb[:, t, :]).then_inc(stats_step, 1)
                dve.wait_ge(stats_step, 1 + (b + 1) * TB)
                for t in range(b * TB, (b + 1) * TB):
                    last = nc.vector.bn_aggr(mean_var[:, t, :], bn[:, t, :])
                last.then_inc(var_ready, 1)

            def normalise(b):
                dve.wait_ge(std_ready, b + 1)
                nc.vector.reciprocal(rstd[:, b * TB:(b + 1) * TB],
                                     std[:, b * TB:(b + 1) * TB]).then_inc(rstd_ready, 1)
                dve.wait_ge(rstd_ready, b + 1)
                for t in range(b * TB, (b + 1) * TB):
                    nc.vector.tensor_scalar(xhat[:, t, :], x_sb[:, t, :], mean_var[:, t, 0:1],
                                            rstd[:, t:t + 1], ALU.subtract, ALU.mult).then_inc(xhat_ready, 1)

            dve.wait_ge(cols_psum, 1)
            nc.vector.tensor_copy(cols[:, :], psum[:, 0, 0:32]).then_inc(cols_ready, 1)
            stats(0)
            dve.wait_ge(cols_ready, 1)
            dve.wait_ge(mod_psum, 1)
            nc.vector.tensor_tensor(t_mod[:, :, :], psum[:, 1, 0:8 * B].rearrange("p (f b) -> p f b", b=B),
                                    cols[:, BT:BT + 8].unsqueeze(2).broadcast_to([P, 8, B]),
                                    ALU.add).then_inc(mod_step, 1)
            dve.wait_ge(mod_step, 1)
            t_mod_v = t_mod[:, :, :].rearrange("p (l s c) b -> p l s c b", l=2, s=2)
            nc.vector.tensor_scalar(mod_one[:, :, :, :], t_mod_v[:, :, 1, :, :], 1.0, None,
                                    ALU.add).then_inc(mod_step, 1)
            dve.wait_ge(mod_step, 2)
            for l in range(2):
                for dst, at in ((mod_mul, LN_W[l]), (mod_add, LN_B[l])):
                    nc.vector.tensor_tensor(dst[:, l, :, :], mod_one[:, l, :, :],
                                            cols[:, at:at + DC].unsqueeze(2).broadcast_to([P, DC, B]),
                                            ALU.mult).then_inc(mod_step, 1)
            dve.wait_ge(mod_step, 6)
            for l in range(2):
                nc.vector.tensor_tensor(mod_add[:, l, :, :], mod_add[:, l, :, :], t_mod_v[:, l, 0, :, :],
                                        ALU.add).then_inc(mod_step, 1)
            normalise(0)

            def rest_part(i):
                kind, b, tg, c = qk_jobs[i]
                at = a_index[qk_jobs[i]]
                dve.wait_ge(high_ready, i + 1)
                if i >= 2:
                    dve.wait_ge(parts_ready, i - 1)
                col = (BQ if kind == "Q" else BK) + c
                nc.vector.scalar_tensor_tensor(
                    out=rest[:, i % 2, :], in0=psum[:, 4 + at % A_RING, :], scalar=cols[:, col:col + 1],
                    in1=parts[:, 3 * (kind == "K"), token_slice(b, c, tg)],
                    op0=ALU.add, op1=ALU.subtract).then_inc(rest_ready, 1)

            def v_out(b, tg, pair):
                at = a_index[("V", b, tg, pair)]
                dve.wait_ge(a_psum, at + 1)
                if b == 0:
                    dve.wait_ge(wv_in, 32)
                    dve.wait_ge(v_ones_made, 1)
                for t in range(2):
                    kc = (4 * tg + 2 * pair + t) % TB
                    dst = v_all[:, b * HG:(b + 1) * HG, kc, :].rearrange("p g (j w) -> p g j w", j=HG)
                    last = nc.vector.tensor_tensor(
                        dst[:, :, :, 0:HD],
                        psum[:, 4 + at % A_RING, t * D:(t + 1) * D].rearrange("p (g j d) -> p g j d", g=HG, j=HG),
                        bv_all[:, :].rearrange("p (g j d) -> p g j d", g=HG, j=HG), ALU.add)
                    last.then_inc(v_ready, 1)

            def tile_max(tile, j, qc):
                dve.wait_ge(smax_psum, tile + 1)
                at = 2 * (qc % 2)
                nc.vector.reduce_max(row_max[:, j % 2, qc:qc + 1],
                                     psum[:, at:at + 2, :].rearrange("p a q -> p (a q)"), AX_X).then_inc(smax_read, 1)

            def negate(head, j):
                dve.wait_ge(smax_read, (head + 1) * TB)
                nc.vector.tensor_scalar(neg_max[:, j % 2, 0, :], row_max[:, j % 2, :], -1.0, None,
                                        ALU.mult).then_inc(neg_high, 1)
                dve.wait_ge(neg_high, head + 1)
                nc.vector.scalar_tensor_tensor(out=neg_max[:, j % 2, 1, :], in0=row_max[:, j % 2, :], scalar=-1.0,
                                               in1=neg_max[:, j % 2, 0, :], op0=ALU.mult,
                                               op1=ALU.subtract).then_inc(neg_ready, 1)

            def first_maxima(tile):
                head, qc = divmod(tile, TB)
                tile_max(tile, head % HG, qc)
                if qc == TB - 1:
                    negate(head, head % HG)

            for i, (kind, b, tg, c) in enumerate(a_jobs):
                for tile in early_tiles(i):
                    first_maxima(tile)
                if kind in "QK":
                    n = qk_jobs.index(a_jobs[i])
                    rest_part(n)
                    if n == 1:
                        stats(1)
                    if n == 4:
                        normalise(1)
                if kind == "V":
                    v_out(b, tg, c)
            for tile in range(early_tiles(len(a_jobs) - 1).stop, (HG + 1) * TB):
                first_maxima(tile)

            def residual(tg):
                for pair in range(2):
                    dve.wait_ge(c_psum, c_index["O", tg, pair] + 1)
                    t = 4 * tg + 2 * pair
                    dve.wait_ge(bo_added, t + 2)
                    nc.vector.tensor_tensor(x_sb[:, t:t + 2, :], psum[:, c_bank("O", tg, pair), :].rearrange("p (t d) -> p t d", d=D),
                                            x_sb[:, t:t + 2, :], ALU.add).then_inc(x1_ready, 1)
                dve.wait_ge(x1_ready, 2 * tg + 2)
                for t in range(4 * tg, 4 * tg + 4):
                    nc.vector.bn_stats(bn[:, t, :], x_sb[:, t, :]).then_inc(stats2_step, 1)
                dve.wait_ge(stats2_step, 4 * tg + 4)
                for t in range(4 * tg, 4 * tg + 4):
                    last = nc.vector.bn_aggr(mean_var[:, t, :], bn[:, t, :])
                last.then_inc(var2_ready, 1)

            def normalise2(b):
                dve.wait_ge(std2_ready, b + 1)
                nc.vector.reciprocal(rstd[:, b * TB:(b + 1) * TB], std[:, b * TB:(b + 1) * TB]).then_inc(rstd2_ready, 1)
                dve.wait_ge(rstd2_ready, b + 1)
                for tg in range(2 * b, 2 * b + 2):
                    if tg >= 2:
                        dve.wait_ge(c_psum, c_index["T", tg - 2, DC - 1] + 1)
                    for t in range(4):
                        at = 4 * tg + t
                        nc.vector.tensor_scalar(xhat2[:, tg % 2, t, :], x_sb[:, at, :], mean_var[:, at, 0:1],
                                                rstd[:, at:at + 1], ALU.subtract, ALU.mult).then_inc(xhat2_ready, 1)

            def early_c_job(kind, tg, c):
                if kind == "O":
                    if c == 1:
                        residual(tg)
                    if c == 1 and tg == 1:
                        normalise2(0)
                    return
                dve.wait_ge(c_psum, c_index[kind, tg, c] + 1)
                src = psum[:, c_bank(kind, tg, c), :]
                if kind == "A":
                    nc.vector.tensor_copy(attn_t[:, tg % 2, c, :], src).then_inc(attn_t_ready, 1)
                else:
                    nc.vector.tensor_scalar(xn2_t[:, c, tg * 512:(tg + 1) * 512], src,
                                            mod_mul[:, 1, c, 0:1], mod_add[:, 1, c, 0:1],
                                            ALU.mult, ALU.add).then_inc(xn2_ready, 1)

            for group in range(NG):
                for step in range(STEPS):
                    ahead = (group + 1) * HG + 1 + step // 4
                    qc = (2 * step) % TB
                    if ahead < NG * HG:
                        tile_max(ahead * TB + qc, ahead % HG, qc)
                        tile_max(ahead * TB + qc + 1, ahead % HG, qc + 1)
                        if step % 4 == 3:
                            negate(ahead, ahead % HG)
                    if step % TB == TB - 1:
                        half = step // TB
                        dve.wait_ge(misc_psum, misc_use(group + 1, 2 * half + 1) + 1 if group + 1 < NG
                                    else misc_use(NG, half))
                        sums = psum[:, MISC_BANK, :].rearrange("p (t j w) -> p t j w", t=4, j=HG)
                        rs = rsum[:, :].rearrange("p (t j) -> p t j", t=4)
                        nc.vector.reciprocal(rs, sums[:, :, :, HD]).then_inc(rsum_ready, 1)
                        dve.wait_ge(rsum_ready, group * 2 + half + 1)
                        dst = attn_out[:, group // 2, 4 * half:4 * half + 4, group % 2, :].rearrange(
                            "p t (j d) -> p t j d", j=HG)
                        nc.vector.tensor_tensor(dst, sums[:, :, :, 0:HD],
                                                rs.unsqueeze(3).broadcast_to([P, 4, HG, HD]),
                                                ALU.mult).then_inc(attn_ready, 1)
                    if group + 1 == NG and step < len(c_early) and c_early[step]:
                        early_c_job(*c_early[step])

            for tg in range(2, 4):
                residual(tg)
            normalise2(1)
            dve.wait_ge(b2_added, NT)
            with dve.Fori(0, TG) as tg:
                for pair in range(2):
                    dve.wait_ge(out_psum, tg * 2 + (pair + 1))
                    rows_of = x_sb[:, bass.ds(tg * 4 + 2 * pair, 2), :]
                    nc.vector.tensor_tensor(rows_of, psum[:, 4 + pair, :].rearrange("p (t d) -> p t d", d=D),
                                            rows_of, ALU.add).then_inc(out_ready, 1)


_INS = ["x", "cond_1024"] + ["L0_cond_" + n for n in (
    "ln1_w", "ln1_b", "ln2_w", "ln2_b", "wq", "bq", "wk", "bk", "wv", "bv", "wo", "bo",
    "wt_attn", "bt_attn", "wt_ffn", "bt_ffn", "w1", "b1", "w2", "b2")]


def kernel(**inputs):
    import numpy as np
    import concourse.bacc as bacc
    from concourse.bass_utils import run_bass_kernel_spmd

    nc = bacc.Bacc("TRN2", target_bir_lowering=False, num_devices=1)
    arrays, args = {}, []
    for name in _INS:
        a = np.ascontiguousarray(inputs[name])
        arrays["in_" + name] = a
        args.append(nc.dram_tensor("in_" + name, a.shape, mybir.dt.from_np(a.dtype), kind="ExternalInput").ap())
    args.append(nc.dram_tensor("out_dram", arrays["in_x"].shape, F32, kind="ExternalOutput").ap())
    layer_program(nc, *args)
    r = run_bass_kernel_spmd(nc, [arrays], core_ids=[0])
    return r.results[0]["out_dram"]
```

```python
from contextlib import ExitStack

import concourse.bass as bass
from concourse import mybir

F32 = mybir.dt.float32
F32R = mybir.dt.float32r
BF16 = mybir.dt.bfloat16
ACT = mybir.ActivationFunctionType
ALU = mybir.AluOpType
AX_X = mybir.AxisListType.X

P = 128
EPS = 1e-5
TERMS = [(0, 0), (0, 1), (1, 0), (0, 2), (2, 0), (1, 1)]

LN_W, LN_B, BQ, BK, BT, B1, COND, B2 = (0, 4), (2, 6), 8, 10, 12, 20, 28, 32
NCOLS = 34


def layer_program(nc, x, cond, ln1_w, ln1_b, ln2_w, ln2_b, wq, bq, wk, bk, wv, bv, wo, bo,
                  wt_attn, bt_attn, wt_ffn, bt_ffn, w1, b1, w2, b2, out):
    B, S, D = x.shape
    F = w1.shape[1]
    H = 16
    HD = D // H
    DC = D // P
    FC = F // P
    NT = B * S // P
    TB = S // P
    HG = 4
    NG = B * H // HG
    VW = HD + 1
    NTERM = len(TERMS)
    KS = NTERM * HD
    SLOTS = 3
    HS = S // 512
    STEPS = HS * TB
    TG = B * S // 512
    SCALE = float(HD) ** -0.5
    assert (D, F, S, B, HD) == (256, 1024, 1024, 2, 16)

    x_tiles = x.rearrange("b (t p) d -> p (b t) d", p=P)
    out_tiles = out.rearrange("b (t p) d -> p (b t) d", p=P)

    with ExitStack() as ctx:
        def sb(name, shape, dt):
            return ctx.enter_context(nc.sbuf_tensor(name, shape, dt))

        def sem(name):
            return ctx.enter_context(nc.semaphore(name))

        x_sb = sb("x_sb", [P, NT, D], F32)
        attn_sb = sb("attn_sb", [P, NG // 2, TB, 2, HG * HD], F32)
        v_group = sb("v_group", [P, TB, HG, 32], F32)
        wq_sb = sb("wq_sb", [P, DC, D], F32)
        wk_sb = sb("wk_sb", [P, DC, D], F32)
        wv_sb = sb("wv_sb", [P, DC, D], F32)
        wo_sb = sb("wo_sb", [P, DC, D], F32)
        w1_sb = sb("w1_sb", [P, DC, F], F32)
        w2_sb = sb("w2_sb", [P, FC, D], F32)
        rows = sb("rows", [NCOLS, P], F32)
        cols = sb("cols", [P, NCOLS], F32)
        bv_all = sb("bv_all", [P, D], F32)
        bo_all = sb("bo_all", [P, D], F32)
        ident = sb("ident", [P, P], F32)
        ident_bf = sb("ident_bf", [P, P], BF16)
        t_mod = sb("t_mod", [P, 8, B], F32)
        mod_one = sb("mod_one", [P, 2, DC, B], F32)
        mod_mul = sb("mod_mul", [P, 2, DC, B], F32)
        mod_add = sb("mod_add", [P, 2, DC, B], F32)
        bn = sb("bn", [P, NT, 6], F32)
        mean_var = sb("mean_var", [P, NT, 2], F32)
        eps_col = sb("eps_col", [P, 1], F32)
        std = sb("std", [P, NT], F32)
        rstd = sb("rstd", [P, NT], F32)
        rest = sb("rest", [P, 2, 512], F32)
        row_max = sb("row_max", [P, 2, TB], F32)
        neg_max = sb("neg_max", [P, 2, 2, TB], BF16)
        neg_max_t = sb("neg_max_t", [16, HG, P], BF16)
        rsum = sb("rsum", [P, 4 * HG], F32)

        with ExitStack() as first_use:
            def sb1(name, shape, dt):
                return first_use.enter_context(nc.sbuf_tensor(name, shape, dt))

            wt_sb = sb1("wt_sb", [P, 2, DC, 2 * D], F32)
            v_all = sb1("v_all", [P, NG, TB, HG * VW], F32)
            work = sb1("work", [P, 4096], F32)
            parts = sb1("parts", [P, 2 * 3, B * DC * S], BF16)
            stack = sb1("stack", [P, SLOTS * HG * 2, S], BF16)

        w1_low = sb("w1_low", [P, DC, F], F32R)
        w2_low = sb("w2_low", [P, FC, D], F32R)
        sb("unused_of_v_all", [P, 8 * D + NG * TB * HG * VW - 2 * DC * F], F32)
        HID_RING = 4
        hid_full = sb("hid_full", [P, HID_RING, 512], F32)
        mlp_out_t = sb("mlp_out_t", [P, DC, 512], F32)
        sb("unused_of_work", [P, 4096 - (HID_RING + DC) * 512], F32)
        w1_high = sb("w1_high", [P, DC, F], F32R)
        w2_high = sb("w2_high", [P, FC, D], F32R)
        attn_t = sb("attn_t", [P, 2, DC, 512], F32)
        xhat2 = sb("xhat2", [P, 2, 4, D], F32)
        xn2_high = sb("xn2_high", [P, DC, TG * 512], F32R)
        after_slot = {name: sb(name, [P, 8 * 512], F32R) for name in
                      sorted(("hid_high", "hid_low", "xn2_low"),
                             key=lambda n: (NG - 3 + ("xn2_low", "hid_high", "hid_low").index(n)) % SLOTS)}
        hid_high = after_slot["hid_high"][:, :].rearrange("p (f t) -> p f t", f=FC)
        hid_low = after_slot["hid_low"][:, :].rearrange("p (f t) -> p f t", f=FC)
        xn2_low = after_slot["xn2_low"][:, :].rearrange("p (c t) -> p c t", c=DC)

        out_t = rest[:, 0, :]
        xn_t = work[:, :].rearrange("p (c t) -> p c t", c=DC)
        probs = work[:, :].rearrange("p (a j q) -> p a j q", a=2, j=HG)
        xhat = attn_sb[:, :, :, :, :].rearrange("p n t o f -> p (n t o f)").rearrange("p (t d) -> p t d", d=D)
        attn_out = attn_sb[:, :, :, :, :]

        psum = ctx.enter_context(nc.psum_tensor("psum", [P, 8, 512], F32))
        ST_BANK, PV_BANK, MISC_BANK = 4, 6, 7

        rows_in, cond_in, wt_in = sem("rows_in"), sem("cond_in"), sem("wt_in")
        x_in = [sem(f"x_in{b}") for b in range(B)]
        wqk_in, wv_in, late_in = sem("wqk_in"), sem("wv_in"), sem("late_in")
        ident_made, ones_made, v_ones_made = sem("ident_made"), sem("ones_made"), sem("v_ones_made")
        cols_psum, cols_ready = sem("cols_psum"), sem("cols_ready")
        mod_psum, mod_step = sem("mod_psum"), sem("mod_step")
        stats_step, var_ready, std_ready, rstd_ready = (
            sem("stats_step"), sem("var_ready"), sem("std_ready"), sem("rstd_ready"))
        xhat_ready, xn_ready = sem("xhat_ready"), sem("xn_ready")
        a_psum = sem("a_psum")
        high_ready, rest_ready, mid_ready, parts_ready = (
            sem("high_ready"), sem("rest_ready"), sem("mid_ready"), sem("parts_ready"))
        v_ready = sem("v_ready")
        stack_in = [sem(f"stack_in{j}") for j in range(HG)]
        smax_psum, smax_read, neg_ready = sem("smax_psum"), sem("smax_read"), sem("neg_ready")
        row_max_done, neg_high = sem("row_max_done"), sem("neg_high")
        misc_psum = sem("misc_psum")
        neg_t_ready = sem("neg_t_ready")
        max_row_in = [sem(f"max_row_in{j}") for j in range(HG)]
        st_psum, probs_ready = sem("st_psum"), sem("probs_ready")
        pv_step = sem("pv_step")
        v_group_ready, out_t_ready = sem("v_group_ready"), sem("out_t_ready")
        rsum_ready, attn_ready = sem("rsum_ready"), sem("attn_ready")
        bo_added, w_high_made, w_split = sem("bo_added"), sem("w_high_made"), sem("w_split")
        c_psum = sem("c_psum")
        attn_t_ready, x1_ready = sem("attn_t_ready"), sem("x1_ready")
        stats2_step, var2_ready, std2_ready, rstd2_ready = (
            sem("stats2_step"), sem("var2_ready"), sem("std2_ready"), sem("rstd2_ready"))
        xhat2_ready, xn2_full_ready, xn2_high_ready, xn2_ready = (
            sem("xhat2_ready"), sem("xn2_full_ready"), sem("xn2_high_ready"), sem("xn2_ready"))
        hid_psum, hid_full_ready, hid_high_ready, hid_ready = (
            sem("hid_psum"), sem("hid_full_ready"), sem("hid_high_ready"), sem("hid_ready"))
        mlp_out_psum, mlp_out_t_ready = sem("mlp_out_psum"), sem("mlp_out_t_ready")
        out_psum, out_ready, out_stored = sem("out_psum"), sem("out_ready"), sem("out_stored")

        a_jobs = []
        for b in range(B):
            tgs = range(b * TG // B, (b + 1) * TG // B)
            a_jobs += [("T", b, tg, c) for tg in tgs for c in range(DC)]
            for c in range(DC):
                a_jobs += [(kind, b, tg, c) for tg in tgs for kind in "QK"]
            a_jobs += [("V", b, tg, pair) for tg in tgs for pair in range(2)]
        A_RING = 3

        def early_tiles(i):
            n = i - len(a_jobs) // B
            return range(2 * n - 2, 2 * n) if n >= 1 else range(0)

        a_index = {job: i for i, job in enumerate(a_jobs)}
        qk_jobs = [job for job in a_jobs if job[0] in "QK"]

        DEV2_STEP = 9

        def jobs(*names):
            return [(name[0], int(name[1]), c) for name in names for c in range(2)]

        c_early = jobs("A0", "A1", "O0", "O1") + [None, None, None] + jobs("T0", "T1")
        c_middle, c_late = jobs("A2", "A3", "O2", "O3"), jobs("T2", "T3")
        c_index = {job: i for i, job in enumerate([x for x in c_early if x] + c_middle + c_late)}

        def c_bank(kind, tg, c):
            if tg < 2:
                return c
            return {"A": 2 * (tg % 2), "O": 4, "T": 6}[kind] + c

        LAST_MAX_STEP = (NG - 1) * STEPS - 4

        def st_bank(tile):
            return (4, 5, 2, 3)[tile % HG] if tile // HG > LAST_MAX_STEP else ST_BANK + tile % 2

        def a_read(i):
            kind, b, tg, c = a_jobs[i]
            if kind == "T":
                return xn_ready, DC * tg + c + 1
            if kind == "V":
                return v_ready, 2 * (2 * tg + c + 1)
            return rest_ready, qk_jobs.index(a_jobs[i]) + 1

        def c_read(kind, tg, c):
            return {"A": attn_t_ready, "O": x1_ready, "T": xn2_full_ready}[kind], 2 * tg + c + 1

        c_order = [x for x in c_early if x] + c_middle + c_late

        def c_before(job):
            return [x for x in c_order[:c_order.index(job)] if c_bank(*x) == c_bank(*job)][-1:]

        def token_slice(b, c, tg):
            at = (b * DC + c) * S + (tg % (TG // B)) * 512
            return slice(at, at + 512)

        def head_in_stack(slot, j, side, first, size):
            return bass.ds(slot + ((2 * j + side) * S + first), size)

        def slot_of(group):
            return (group % SLOTS) * (HG * 2 * S)

        def misc_use(group, j):
            return j + 1 if group == 0 else HG + 6 * (group - 1) + j + 1 + (j >= 2)

        stack_flat = stack[:, :, :].rearrange("p a t -> p (a t)")
        parts_flat = parts[:, :, :]

        block = ctx.enter_context(nc.Block())

        @block.sync
        def _(sp):
            for at, vec in ((0, ln1_w), (2, ln1_b), (4, ln2_w), (6, ln2_b), (8, bq), (10, bk),
                            (12, bt_attn), (16, bt_ffn), (20, b1), (32, b2)):
                r = vec.rearrange("(r k) -> r k", k=P)
                sp.dma_start(rows[at:at + r.shape[0], :], r).then_inc(rows_in, 16)
            sp.dma_start(rows[28:32, :], cond.rearrange("b (c k) -> (b c) k", k=P)).then_inc(rows_in, 16)
            sp.dma_start(x_sb[:, TB:2 * TB, :], x_tiles[:, TB:2 * TB, :]).then_inc(x_in[1], 16)
            sp.dma_start(wv_sb[:, :, :], wv.rearrange("(c k) n -> k c n", k=P)).then_inc(wv_in, 16)
            sp.dma_start(bv_all[:, :], bv.partition_broadcast(P)).then_inc(wv_in, 16)
            for dst, src in ((wo_sb, wo), (w1_sb, w1), (w2_sb, w2)):
                sp.dma_start(dst[:, :, :], src.rearrange("(c k) n -> k c n", k=P)).then_inc(late_in, 16)
            for dst, src in ((bo_all, bo),):
                sp.dma_start(dst[:, :], src.partition_broadcast(P)).then_inc(late_in, 16)

            def load_head(group, pair, odd, j):
                p0 = 64 * odd + 16 * j
                slot = (group % SLOTS) * (HG * 2)
                for t, (a, b) in enumerate(TERMS):
                    src = parts_flat[p0:p0 + HD, a:4 + b:3 + b - a, bass.ds(pair * S, S)]
                    at = slot + 2 * j
                    sp.dma_start(stack[t * HD:(t + 1) * HD, bass.ds(at, 2), :], src).then_inc(stack_in[j], 16)

            def store_max(group, j):
                slot = slot_of(group)
                sp.wait_ge(neg_t_ready, 4 * group + j + 1)
                for part in range(2):
                    sp.dma_start(stack_flat[KS + part:KS + part + 1, head_in_stack(slot, j, 0, 0, S)],
                                 neg_max_t[part * TB:(part + 1) * TB, j, :]).then_inc(max_row_in[j], 16)

            sp.wait_ge(parts_ready, 4)
            for j in range(HG):
                load_head(0, 0, 0, j)
            for j in range(HG):
                sp.wait_ge(stack_in[j], 16 * NTERM)
                load_head(1, 0, 1, j)
                store_max(0, j)
            sp.wait_ge(parts_ready, len(qk_jobs))
            for group in range(2, NG):
                sp.wait_ge(st_psum, (group - 2) * (STEPS * HG) + 1)
                for j in range(HG):
                    sp.wait_ge(stack_in[j], 16 * NTERM * group)
                    load_head(group, group // 2, group % 2, j)
                    store_max(group - 1, j)
            for j in range(HG):
                store_max(NG - 1, j)
            with sp.Fori(0, TG) as tg:
                for pair in range(2):
                    sp.wait_ge(out_ready, 2 + tg * 2 + (pair + 1))
                    sp.dma_start(out_tiles[:, bass.ds(tg * 4 + 2 * pair, 2), :],
                                 x_sb[:, bass.ds(tg * 4 + 2 * pair, 2), :]).then_inc(out_stored, 16)
            sp.wait_ge(out_stored, 16 * 2 * TG)

        @block.gpsimd
        def _(pool):
            nc.gpsimd.memset(ident[:, :], 0.0).then_inc(ident_made, 1)
            pool.wait_ge(ident_made, 1)
            nc.gpsimd.affine_select(out=ident[:, :], in_=ident[:, :], compare_op=ALU.not_equal, fill=1.0,
                                    base=0, pattern=[[-1, P]], channel_multiplier=1).then_inc(ident_made, 1)
            pool.wait_ge(ident_made, 2)
            nc.gpsimd.tensor_copy(ident_bf[:, :], ident[:, :]).then_inc(ident_made, 1)
            nc.gpsimd.memset(v_all[:, :, :, :], 1.0).then_inc(v_ones_made, 1)
            nc.gpsimd.memset(v_group[:, :, :, :], 0.0).then_inc(v_ones_made, 1)
            pool.wait_ge(v_ones_made, 2)
            for s in range(SLOTS):
                sides = stack[KS:P, s * HG * 2:(s + 1) * HG * 2, :]
                nc.gpsimd.memset(sides[:, 1::2, :], 1.0).then_inc(ones_made, 1)
            pool.wait_ge(ones_made, SLOTS)
            for i, (kind, b, tg, c) in enumerate(qk_jobs):
                side = 3 * (kind == "K")
                pool.wait_ge(mid_ready, i + 1)
                nc.gpsimd.tensor_tensor(parts[:, side + 2, token_slice(b, c, tg)], rest[:, i % 2, :],
                                        parts[:, side + 1, token_slice(b, c, tg)],
                                        ALU.subtract).then_inc(parts_ready, 1)

            def fill_v(group, half):
                nc.gpsimd.tensor_copy(
                    v_group[:, half * 4:half * 4 + 4, :, 0:VW],
                    v_all[:, bass.ds(group, 1), half * 4:half * 4 + 4, :].rearrange(
                        "p n k (j w) -> p (n k) j w", j=HG)).then_inc(v_group_ready, 1)

            pool.wait_ge(v_ready, 8)
            pool.wait_ge(v_ones_made, 2)
            for half in range(2):
                fill_v(0, half)
            pool.wait_ge(late_in, 16 * 4)
            for t in range(NT):
                nc.gpsimd.tensor_tensor(x_sb[:, t, :], x_sb[:, t, :], bo_all[:, :], ALU.add).then_inc(bo_added, 1)
            def refill_v(group):
                for half in range(2):
                    pool.wait_ge(pv_step, group * STEPS - (4 - 4 * half))
                    fill_v(group, half)

            with pool.Fori(1, NG - 1) as group:
                refill_v(group)
            for j in range(HG):
                pool.wait_ge(stack_in[j], 16 * NTERM * NG)
            def split_weight(i, high, low, w):
                nc.gpsimd.tensor_copy(high[:, :, :], w[:, :, :]).then_inc(w_high_made, 1)
                pool.wait_ge(w_high_made, i + 1)
                nc.gpsimd.tensor_tensor(low[:, :, :], w[:, :, :], high[:, :, :], ALU.subtract).then_inc(w_split, 1)

            split_weight(0, w1_high, w1_low, w1_sb)
            refill_v(NG - 1)
            pool.wait_ge(v_group_ready, 2 * NG)
            split_weight(1, w2_high, w2_low, w2_sb)

        @block.tensor
        def _(pe):
            pe.wait_ge(ident_made, 2)
            pe.wait_ge(rows_in, 16 * 11)
            nc.tensor.transpose(psum[:, 0, 0:NCOLS], rows[:, :], ident[0:NCOLS, 0:NCOLS]).then_inc(cols_psum, 1)
            pe.wait_ge(cols_ready, 1)
            pe.wait_ge(wt_in, 32)
            for which in range(2):
                for f in range(4):
                    for c in range(DC):
                        last = nc.tensor.matmul(psum[:, 1, (4 * which + f) * B:(4 * which + f + 1) * B],
                                                wt_sb[:, which, c, f * P:(f + 1) * P],
                                                cols[:, COND + c:COND + c + 3:2],
                                                start=(c == 0), stop=(c == DC - 1))
            last.then_inc(mod_psum, 1)

            def scores_for_max(tile, slot, j, qc, half):
                if half == 0 and tile >= 2:
                    pe.wait_ge(smax_read, tile - 1)
                last = nc.tensor.matmul(
                    psum[:, 2 * (qc % 2) + half, :],
                    stack_flat[0:KS, head_in_stack(slot, j, 0, qc * P, P)],
                    stack_flat[0:KS, head_in_stack(slot, j, 1, half * 512, 512)],
                    start=True, stop=True)
                if half == 1:
                    last.then_inc(smax_psum, 1)

            def turn_max(head, j):
                if head:
                    pe.wait_ge(neg_t_ready, head)
                pe.wait_ge(neg_ready, head + 1)
                nc.tensor.transpose(psum[0:16, MISC_BANK, 0:64].bitcast(BF16),
                                    neg_max[:, j % 2, :, :].rearrange("p a t -> p (a t)"),
                                    ident_bf[:, :]).then_inc(misc_psum, 1)

            def scores_for_exp(slot, step, j, tile):
                half, kc = divmod(step, TB)
                same = [u for u in range(max(tile - HG, 0), tile) if st_bank(u) == st_bank(tile)]
                if same:
                    pe.wait_ge(probs_ready, same[-1] + 1)
                elif tile > HG:
                    pe.wait_ge(smax_read, NG * HG * TB)
                last = nc.tensor.matmul(
                    psum[:, st_bank(tile), :],
                    stack_flat[0:KS + 2, head_in_stack(slot, j, 1, kc * P, P)],
                    stack_flat[0:KS + 2, head_in_stack(slot, j, 0, half * 512, 512)],
                    start=True, stop=True)
                last.then_inc(st_psum, 1)
                return last

            def first_maxima(tile):
                head, qc = divmod(tile, TB)
                if qc == 0:
                    pe.wait_ge(stack_in[head % HG], 16 * NTERM * (head // HG + 1))
                for half in range(2):
                    scores_for_max(tile, slot_of(head // HG), head % HG, qc, half)
                if qc == 3 and head:
                    turn_max(head - 1, head - 1)

            pe.wait_ge(ident_made, 3)
            for i, (kind, b, tg, c) in enumerate(a_jobs):
                for tile in early_tiles(i):
                    first_maxima(tile)
                bank = 4 + i % A_RING
                if i >= A_RING:
                    pe.wait_ge(*a_read(i - A_RING))
                if kind == "T":
                    pe.wait_ge(xhat_ready, 4 * tg + 4)
                    for t in range(4):
                        last = nc.tensor.transpose(psum[:, bank, t * P:(t + 1) * P],
                                                   xhat[:, 4 * tg + t, c * P:(c + 1) * P], ident[:, :])
                    last.then_inc(a_psum, 1)
                    continue
                pe.wait_ge(xn_ready, DC * (tg + 1))
                if kind in "QK":
                    pe.wait_ge(wqk_in, 32)
                    w = wq_sb if kind == "Q" else wk_sb
                    for k in range(DC):
                        last = nc.tensor.matmul(psum[:, bank, :], w[:, k, c * P:(c + 1) * P],
                                                xn_t[:, k, tg * 512:(tg + 1) * 512],
                                                start=(k == 0), stop=(k == DC - 1))
                else:
                    pe.wait_ge(wv_in, 32)
                    for t in range(2):
                        token = (4 * tg + 2 * c + t) * P
                        for k in range(DC):
                            last = nc.tensor.matmul(psum[:, bank, t * D:(t + 1) * D],
                                                    xn_t[:, k, token:token + P], wv_sb[:, k, :],
                                                    start=(k == 0), stop=(k == DC - 1))
                last.then_inc(a_psum, 1)

            for tile in range(early_tiles(len(a_jobs) - 1).stop, (HG + 1) * TB):
                first_maxima(tile)
            for i in range(len(a_jobs) - A_RING, len(a_jobs)):
                pe.wait_ge(*a_read(i))
            pe.wait_ge(ones_made, SLOTS)
            for j in range(HG):
                pe.wait_ge(max_row_in[j], 32)
                scores_for_exp(0, 0, j, j)

            def c_job(kind, tg, c):
                bank = c_bank(kind, tg, c)
                for job in c_before((kind, tg, c)):
                    pe.wait_ge(*c_read(*job))
                if kind == "A":
                    for t in range(4):
                        b, tb = divmod(4 * tg + t, TB)
                        last = nc.tensor.transpose(
                            psum[:, bank, t * P:(t + 1) * P],
                            attn_out[:, b * DC + c, tb, :, :].rearrange("p o f -> p (o f)"), ident[:, :])
                elif kind == "O":
                    pe.wait_ge(attn_t_ready, DC * (tg + 1))
                    for t in range(2):
                        at = (2 * c + t) * P
                        for k in range(DC):
                            last = nc.tensor.matmul(psum[:, bank, t * D:(t + 1) * D],
                                                    attn_t[:, tg % 2, k, at:at + P], wo_sb[:, k, :],
                                                    start=(k == 0), stop=(k == DC - 1))
                else:
                    pe.wait_ge(xhat2_ready, 4 * (tg + 1))
                    for t in range(4):
                        last = nc.tensor.transpose(psum[:, bank, t * P:(t + 1) * P],
                                                   xhat2[:, tg % 2, t, c * P:(c + 1) * P], ident[:, :])
                last.then_inc(c_psum, 1)

            def three_products(out, w, x, first, last):
                for i, (a, b) in enumerate(((0, 0), (0, 1), (1, 0))):
                    mm = nc.tensor.matmul(out, w[a], x[b], start=first and i == 0, stop=last and i == 2)
                return mm

            def mlp_hidden(tg, back=False):
                for f in range(FC):
                    if f >= 4:
                        pe.wait_ge(hid_full_ready, tg * FC + (f - 3))
                    tokens, hidden = bass.ds(tg * 512, 512), slice(f * P, (f + 1) * P)
                    for k in range(DC):
                        last = three_products(psum[:, f % 4, :], (w1_high[:, k, hidden], w1_low[:, k, hidden]),
                                              (xn2_high[:, k, tokens], xn2_low[:, k, tokens]),
                                              k == 0, k == DC - 1)
                    last.then_inc(hid_psum, 1)
                    if f == 1 and back:
                        mlp_back(tg - 1)

            def mlp_output(tg, wait=True):
                if wait:
                    pe.wait_ge(mlp_out_t_ready, tg * DC)
                for f in range(FC):
                    pe.wait_ge(hid_ready, tg * FC + (f + 1))
                    for c in range(DC):
                        feats = slice(c * P, (c + 1) * P)
                        last = three_products(psum[:, 4 + c, :], (w2_high[:, f, feats], w2_low[:, f, feats]),
                                              (hid_high[:, f, :], hid_low[:, f, :]), f == 0, f == FC - 1)
                        if f == FC - 1:
                            last.then_inc(mlp_out_psum, 1)

            def mlp_back(tg):
                pe.wait_ge(mlp_out_t_ready, (tg + 1) * DC)
                for pair in range(2):
                    pe.wait_ge(out_ready, tg * 2 + (pair + 1))
                    for t in range(2):
                        for c in range(DC):
                            at = (2 * pair + t) * P
                            last = nc.tensor.transpose(psum[:, 6 + pair, t * D + c * P:t * D + (c + 1) * P],
                                                       mlp_out_t[:, c, at:at + P], ident[:, :])
                    last.then_inc(out_psum, 1)

            def group_steps(group):
                more = group + 1 < NG
                slot, next_slot = slot_of(group), slot_of(group + 1)
                for step in range(STEPS):
                    ahead = (group + 1) * HG + 1 + step // 4
                    ahead_group, ahead_j = divmod(ahead, HG)
                    qc = (2 * step) % TB
                    last_of_group = step + 1 == STEPS

                    def next_scores(j):
                        if last_of_group and not more:
                            return
                        if last_of_group:
                            pe.wait_ge(max_row_in[j], 32 * (group + 2))
                        scores_for_exp(next_slot if last_of_group else slot, (step + 1) % STEPS, j,
                                       (group * STEPS + step + 1) * HG + j)

                    def max_scores(tile, half):
                        if ahead < NG * HG:
                            scores_for_max(ahead * TB + qc + tile, slot_of(ahead_group), ahead_j, qc + tile, half)

                    if step % 4 == 0 and ahead < NG * HG:
                        pe.wait_ge(stack_in[ahead_j], 16 * NTERM * (ahead_group + 1))
                    max_scores(0, 0)
                    next_scores(0)
                    max_scores(0, 1)
                    next_scores(1)
                    pe.wait_ge(probs_ready, (group * STEPS + step + 1) * HG)
                    if step == 0 or step == 4:
                        pe.wait_ge(v_group_ready, group * 2 + 1 + step // 4)
                    if step % TB == 0 and (group or step):
                        pe.wait_ge(out_t_ready, group * 2 + step // TB)
                    for j in range(HG):
                        last = nc.tensor.matmul(psum[32 * j:32 * j + 32, PV_BANK, :],
                                                v_group[:, step % TB, j, :], probs[:, step % 2, j, :],
                                                start=(step % TB == 0), stop=(step % TB == TB - 1))
                    last.then_inc(pv_step, 1)
                    next_scores(2)
                    max_scores(1, 0)
                    next_scores(3)
                    max_scores(1, 1)
                    if step % 4 == 0 and more:
                        if step % TB == 0 and (group or step):
                            pe.wait_ge(attn_ready, group * 2 + step // TB)
                        turn_max((group + 1) * HG + step // 4, step // 4)
                    if step % TB == TB - 1:
                        half = step // TB
                        if more:
                            pe.wait_ge(neg_t_ready, (group + 1) * HG + 2 * half + 2)
                        else:
                            pe.wait_ge(attn_ready, group * 2 + half)
                        pe.wait_ge(out_t_ready, group * 2 + half + 1)
                        for t in range(4):
                            last = nc.tensor.transpose(psum[:, MISC_BANK, t * P:(t + 1) * P],
                                                       out_t[:, t * P:(t + 1) * P], ident[:, :])
                        last.then_inc(misc_psum, 1)
                    if not more and step < len(c_early) and c_early[step]:
                        if step == 0:
                            pe.wait_ge(smax_read, NG * HG * TB)
                            pe.wait_ge(attn_ready, NG)
                            pe.wait_ge(late_in, 16 * 4)
                        c_job(*c_early[step])

            for group in range(NG):
                group_steps(group)

            pe.wait_ge(attn_ready, 2 * NG)
            for job in c_middle:
                c_job(*job)
            pe.wait_ge(attn_t_ready, DC * TG)
            pe.wait_ge(x1_ready, 2 * TG)
            pe.wait_ge(xn2_ready, DC * 2)
            pe.wait_ge(w_split, 2)
            mlp_hidden(0)
            for job in c_late:
                c_job(*job)
            mlp_output(0, wait=False)
            pe.wait_ge(xn2_ready, DC * TG)
            with pe.Fori(1, TG) as tg:
                mlp_hidden(tg, back=True)
                mlp_output(tg)
            mlp_back(TG - 1)

        @block.scalar
        def _(act):
            act.dma_start(x_sb[:, 0:TB, :], x_tiles[:, 0:TB, :]).then_inc(x_in[0], 16)
            for which, w in enumerate((wt_attn, wt_ffn)):
                act.dma_start(wt_sb[:, which, :, :], w.rearrange("(c k) n -> k c n", k=P)).then_inc(wt_in, 16)
            for dst, src in ((wq_sb, wq), (wk_sb, wk)):
                act.dma_start(dst[:, :, :], src.rearrange("(c k) n -> k c n", k=P)).then_inc(wqk_in, 16)

            def deviation(b):
                act.wait_ge(var_ready, b + 1)
                nc.scalar.activation(std[:, b * TB:(b + 1) * TB], mean_var[:, b * TB:(b + 1) * TB, 1],
                                     ACT.Sqrt, bias=eps_col[:, 0:1]).then_inc(std_ready, 1)

            def xn_out(tg, c, b):
                i = a_index[("T", b, tg, c)]
                act.wait_ge(a_psum, i + 1)
                nc.scalar.activation(xn_t[:, c, tg * 512:(tg + 1) * 512], psum[:, 4 + i % A_RING, :], ACT.Identity,
                                     bias=mod_add[:, 0, c, b:b + 1],
                                     scale=mod_mul[:, 0, c, b:b + 1]).then_inc(xn_ready, 1)

            def high_part(i):
                kind, b, tg, c = qk_jobs[i]
                at = a_index[qk_jobs[i]]
                act.wait_ge(a_psum, at + 1)
                col = (BQ if kind == "Q" else BK) + c
                nc.scalar.activation(parts[:, 3 * (kind == "K"), token_slice(b, c, tg)], psum[:, 4 + at % A_RING, :],
                                     ACT.Identity, bias=cols[:, col:col + 1]).then_inc(high_ready, 1)

            def middle_part(i):
                kind, b, tg, c = qk_jobs[i]
                act.wait_ge(rest_ready, i + 1)
                nc.scalar.copy(parts[:, 3 * (kind == "K") + 1, token_slice(b, c, tg)],
                               rest[:, i % 2, :]).then_inc(mid_ready, 1)

            def turned_max(group, j):
                act.wait_ge(misc_psum, misc_use(group, j))
                if group:
                    act.wait_ge(max_row_in[j], 32 * group)
                nc.scalar.copy(neg_max_t[:, j, :], psum[0:16, MISC_BANK, 0:64].bitcast(BF16)).then_inc(neg_t_ready, 1)

            def first_turned(tile):
                if tile % TB == 3 and tile > TB:
                    turned_max(0, tile // TB - 1)

            deviation(0)
            act.wait_ge(mod_step, 8)
            for i, (kind, b, tg, c) in enumerate(a_jobs):
                for tile in early_tiles(i):
                    first_turned(tile)
                if kind == "T":
                    xn_out(tg, c, b)
                if kind in "QK":
                    n = qk_jobs.index(a_jobs[i])
                    high_part(n)
                    if n % (len(qk_jobs) // B):
                        middle_part(n - 1)
                    if n == 2:
                        deviation(1)
                if kind == "V" and tg % (TG // B) == 0 and c == 0:
                    middle_part((b + 1) * len(qk_jobs) // B - 1)
            for tile in range(early_tiles(len(a_jobs) - 1).stop, (HG + 1) * TB):
                first_turned(tile)

            def exponentials(tile):
                act.wait_ge(st_psum, tile + 1)
                nc.scalar.activation(probs[:, tile // HG % 2, tile % HG, :], psum[:, st_bank(tile), :], ACT.Exp,
                                     scale=SCALE).then_inc(probs_ready, 1)

            act.wait_ge(a_psum, len(a_jobs))
            def deviation2(b):
                act.wait_ge(var2_ready, 2 * b + 2)
                nc.scalar.activation(std[:, b * TB:(b + 1) * TB], mean_var[:, b * TB:(b + 1) * TB, 1],
                                     ACT.Sqrt, bias=eps_col[:, 0:1]).then_inc(std2_ready, 1)

            for j in range(HG):
                exponentials(j)
            for group in range(NG):
                more = group + 1 < NG
                for step in range(STEPS):
                    for j in range(HG):
                        if step + 1 < STEPS or more:
                            if j == 0 and (group or step):
                                act.wait_ge(pv_step, group * STEPS + step)
                            exponentials((group * STEPS + step + 1) * HG + j)
                        if j == 1 and step % 4 == 1 and more:
                            turned_max(group + 1, step // 4)
                        if j == 1 and step == DEV2_STEP and not more:
                            deviation2(0)
                        if step % TB == TB - 1 and j == 1:
                            half = step // TB
                            act.wait_ge(pv_step, group * STEPS + step + 1)
                            if group or half:
                                act.wait_ge(attn_ready, group * 2 + half)
                            nc.scalar.copy(out_t, psum[:, PV_BANK, :]).then_inc(out_t_ready, 1)

            def c_job(kind, tg, c):
                act.wait_ge(c_psum, c_index[kind, tg, c] + 1)
                src = psum[:, c_bank(kind, tg, c), :]
                if kind == "A":
                    nc.scalar.copy(attn_t[:, tg % 2, c, :], src).then_inc(attn_t_ready, 1)
                else:
                    act.wait_ge(xn2_ready, DC * tg + c - 1)
                    b = tg * B // TG
                    nc.scalar.activation(rest[:, c, :], src, ACT.Identity,
                                         bias=mod_add[:, 1, c, b:b + 1],
                                         scale=mod_mul[:, 1, c, b:b + 1]).then_inc(xn2_full_ready, 1)

            def hidden(tg, first=False):
                for f in range(FC):
                    act.wait_ge(hid_psum, tg * FC + (f + 1))
                    if f >= HID_RING or not first:
                        act.wait_ge(hid_ready, tg * FC + (f + 1 - HID_RING))
                    nc.scalar.activation(hid_full[:, f % HID_RING, :], psum[:, f % 4, :], ACT.Gelu,
                                         bias=cols[:, B1 + f:B1 + f + 1]).then_inc(hid_full_ready, 1)

            def output(tg, first=False):
                for c in range(DC):
                    act.wait_ge(mlp_out_psum, tg * DC + (c + 1))
                    if c == 0 and not first:
                        act.wait_ge(out_psum, tg * 2)
                    nc.scalar.activation(mlp_out_t[:, c, :], psum[:, 4 + c, :], ACT.Identity,
                                         bias=cols[:, B2 + c:B2 + c + 1]).then_inc(mlp_out_t_ready, 1)

            for job in c_middle[:4]:
                c_job(*job)
            deviation2(1)
            hidden(0, first=True)
            for job in c_late:
                c_job(*job)
            output(0, first=True)
            with act.Fori(1, TG) as tg:
                hidden(tg)
                output(tg)

        @block.vector
        def _(dve):
            nc.vector.memset(eps_col[:, :], EPS).then_inc(stats_step, 1)
            nc.vector.memset(rsum[:, :], 0.0).then_inc(out_ready, 2)

            def stats(b):
                dve.wait_ge(x_in[b], 16)
                for t in range(b * TB, (b + 1) * TB):
                    nc.vector.bn_stats(bn[:, t, :], x_sb[:, t, :]).then_inc(stats_step, 1)
                dve.wait_ge(stats_step, 1 + (b + 1) * TB)
                for t in range(b * TB, (b + 1) * TB):
                    last = nc.vector.bn_aggr(mean_var[:, t, :], bn[:, t, :])
                last.then_inc(var_ready, 1)

            def normalise(b):
                dve.wait_ge(std_ready, b + 1)
                nc.vector.reciprocal(rstd[:, b * TB:(b + 1) * TB],
                                     std[:, b * TB:(b + 1) * TB]).then_inc(rstd_ready, 1)
                dve.wait_ge(rstd_ready, b + 1)
                for t in range(b * TB, (b + 1) * TB):
                    nc.vector.tensor_scalar(xhat[:, t, :], x_sb[:, t, :], mean_var[:, t, 0:1],
                                            rstd[:, t:t + 1], ALU.subtract, ALU.mult).then_inc(xhat_ready, 1)

            dve.wait_ge(cols_psum, 1)
            nc.vector.tensor_copy(cols[:, :], psum[:, 0, 0:NCOLS]).then_inc(cols_ready, 1)
            stats(0)
            dve.wait_ge(cols_ready, 1)
            dve.wait_ge(mod_psum, 1)
            nc.vector.tensor_tensor(t_mod[:, :, :], psum[:, 1, 0:8 * B].rearrange("p (f b) -> p f b", b=B),
                                    cols[:, BT:BT + 8].unsqueeze(2).broadcast_to([P, 8, B]),
                                    ALU.add).then_inc(mod_step, 1)
            dve.wait_ge(mod_step, 1)
            t_mod_v = t_mod[:, :, :].rearrange("p (l s c) b -> p l s c b", l=2, s=2)
            nc.vector.tensor_scalar(mod_one[:, :, :, :], t_mod_v[:, :, 1, :, :], 1.0, None,
                                    ALU.add).then_inc(mod_step, 1)
            dve.wait_ge(mod_step, 2)
            for l in range(2):
                for dst, at in ((mod_mul, LN_W[l]), (mod_add, LN_B[l])):
                    nc.vector.tensor_tensor(dst[:, l, :, :], mod_one[:, l, :, :],
                                            cols[:, at:at + DC].unsqueeze(2).broadcast_to([P, DC, B]),
                                            ALU.mult).then_inc(mod_step, 1)
            dve.wait_ge(mod_step, 6)
            for l in range(2):
                nc.vector.tensor_tensor(mod_add[:, l, :, :], mod_add[:, l, :, :], t_mod_v[:, l, 0, :, :],
                                        ALU.add).then_inc(mod_step, 1)
            normalise(0)

            def rest_part(i):
                kind, b, tg, c = qk_jobs[i]
                at = a_index[qk_jobs[i]]
                dve.wait_ge(high_ready, i + 1)
                if i >= 2:
                    dve.wait_ge(parts_ready, i - 1)
                col = (BQ if kind == "Q" else BK) + c
                nc.vector.scalar_tensor_tensor(
                    out=rest[:, i % 2, :], in0=psum[:, 4 + at % A_RING, :], scalar=cols[:, col:col + 1],
                    in1=parts[:, 3 * (kind == "K"), token_slice(b, c, tg)],
                    op0=ALU.add, op1=ALU.subtract).then_inc(rest_ready, 1)

            def v_out(b, tg, pair):
                at = a_index[("V", b, tg, pair)]
                dve.wait_ge(a_psum, at + 1)
                if b == 0:
                    dve.wait_ge(wv_in, 32)
                    dve.wait_ge(v_ones_made, 1)
                for t in range(2):
                    kc = (4 * tg + 2 * pair + t) % TB
                    dst = v_all[:, b * HG:(b + 1) * HG, kc, :].rearrange("p g (j w) -> p g j w", j=HG)
                    last = nc.vector.tensor_tensor(
                        dst[:, :, :, 0:HD],
                        psum[:, 4 + at % A_RING, t * D:(t + 1) * D].rearrange("p (g j d) -> p g j d", g=HG, j=HG),
                        bv_all[:, :].rearrange("p (g j d) -> p g j d", g=HG, j=HG), ALU.add)
                    last.then_inc(v_ready, 1)

            def tile_max(tile, j, qc):
                dve.wait_ge(smax_psum, tile + 1)
                at = 2 * (qc % 2)
                nc.vector.reduce_max(row_max[:, j % 2, qc:qc + 1],
                                     psum[:, at:at + 2, :].rearrange("p a q -> p (a q)"), AX_X).then_inc(smax_read, 1)

            def negate(head, j):
                dve.wait_ge(smax_read, (head + 1) * TB)
                nc.vector.tensor_scalar(neg_max[:, j % 2, 0, :], row_max[:, j % 2, :], -1.0, None,
                                        ALU.mult).then_inc(neg_high, 1)
                dve.wait_ge(neg_high, head + 1)
                nc.vector.scalar_tensor_tensor(out=neg_max[:, j % 2, 1, :], in0=row_max[:, j % 2, :], scalar=-1.0,
                                               in1=neg_max[:, j % 2, 0, :], op0=ALU.mult,
                                               op1=ALU.subtract).then_inc(neg_ready, 1)

            def first_maxima(tile):
                head, qc = divmod(tile, TB)
                tile_max(tile, head % HG, qc)
                if qc == TB - 1:
                    negate(head, head % HG)

            for i, (kind, b, tg, c) in enumerate(a_jobs):
                for tile in early_tiles(i):
                    first_maxima(tile)
                if kind in "QK":
                    n = qk_jobs.index(a_jobs[i])
                    rest_part(n)
                    if n == 1:
                        stats(1)
                    if n == 4:
                        normalise(1)
                if kind == "V":
                    v_out(b, tg, c)
            for tile in range(early_tiles(len(a_jobs) - 1).stop, (HG + 1) * TB):
                first_maxima(tile)

            def residual(tg):
                for pair in range(2):
                    dve.wait_ge(c_psum, c_index["O", tg, pair] + 1)
                    t = 4 * tg + 2 * pair
                    dve.wait_ge(bo_added, t + 2)
                    nc.vector.tensor_tensor(x_sb[:, t:t + 2, :], psum[:, c_bank("O", tg, pair), :].rearrange("p (t d) -> p t d", d=D),
                                            x_sb[:, t:t + 2, :], ALU.add).then_inc(x1_ready, 1)
                dve.wait_ge(x1_ready, 2 * tg + 2)
                for t in range(4 * tg, 4 * tg + 4):
                    nc.vector.bn_stats(bn[:, t, :], x_sb[:, t, :]).then_inc(stats2_step, 1)
                dve.wait_ge(stats2_step, 4 * tg + 4)
                for t in range(4 * tg, 4 * tg + 4):
                    last = nc.vector.bn_aggr(mean_var[:, t, :], bn[:, t, :])
                last.then_inc(var2_ready, 1)

            def normalise2(b):
                dve.wait_ge(std2_ready, b + 1)
                nc.vector.reciprocal(rstd[:, b * TB:(b + 1) * TB], std[:, b * TB:(b + 1) * TB]).then_inc(rstd2_ready, 1)
                dve.wait_ge(rstd2_ready, b + 1)
                for tg in range(2 * b, 2 * b + 2):
                    if tg >= 2:
                        dve.wait_ge(c_psum, c_index["T", tg - 2, DC - 1] + 1)
                    for t in range(4):
                        at = 4 * tg + t
                        nc.vector.tensor_scalar(xhat2[:, tg % 2, t, :], x_sb[:, at, :], mean_var[:, at, 0:1],
                                                rstd[:, at:at + 1], ALU.subtract, ALU.mult).then_inc(xhat2_ready, 1)

            def split_xn2(tg, c, buffer):
                n, tokens = DC * tg + c, slice(tg * 512, (tg + 1) * 512)
                dve.wait_ge(xn2_full_ready, n + 1)
                nc.vector.tensor_copy(xn2_high[:, c, tokens], rest[:, buffer, :]).then_inc(xn2_high_ready, 1)
                dve.wait_ge(xn2_high_ready, n + 1)
                nc.vector.tensor_tensor(xn2_low[:, c, tokens], rest[:, buffer, :], xn2_high[:, c, tokens],
                                        ALU.subtract).then_inc(xn2_ready, 1)

            def early_c_job(kind, tg, c):
                if kind == "O":
                    if c == 1:
                        residual(tg)
                    if c == 1 and tg == 1:
                        normalise2(0)
                    return
                dve.wait_ge(c_psum, c_index[kind, tg, c] + 1)
                src = psum[:, c_bank(kind, tg, c), :]
                if kind == "A":
                    nc.vector.tensor_copy(attn_t[:, tg % 2, c, :], src).then_inc(attn_t_ready, 1)
                else:
                    if DC * tg + c:
                        dve.wait_ge(xn2_ready, DC * tg + c)
                    nc.vector.tensor_scalar(rest[:, 1, :], src, mod_mul[:, 1, c, 0:1], mod_add[:, 1, c, 0:1],
                                            ALU.mult, ALU.add).then_inc(xn2_full_ready, 1)
                    split_xn2(tg, c, 1)

            for group in range(NG):
                for step in range(STEPS):
                    ahead = (group + 1) * HG + 1 + step // 4
                    qc = (2 * step) % TB
                    if ahead < NG * HG:
                        tile_max(ahead * TB + qc, ahead % HG, qc)
                        tile_max(ahead * TB + qc + 1, ahead % HG, qc + 1)
                        if step % 4 == 3:
                            negate(ahead, ahead % HG)
                    if step % TB == TB - 1:
                        half = step // TB
                        dve.wait_ge(misc_psum, misc_use(group + 1, 2 * half + 1) + 1 if group + 1 < NG
                                    else misc_use(NG, half))
                        sums = psum[:, MISC_BANK, :].rearrange("p (t j w) -> p t j w", t=4, j=HG)
                        rs = rsum[:, :].rearrange("p (t j) -> p t j", t=4)
                        nc.vector.reciprocal(rs, sums[:, :, :, HD]).then_inc(rsum_ready, 1)
                        dve.wait_ge(rsum_ready, group * 2 + half + 1)
                        dst = attn_out[:, group // 2, 4 * half:4 * half + 4, group % 2, :].rearrange(
                            "p t (j d) -> p t j d", j=HG)
                        nc.vector.tensor_tensor(dst, sums[:, :, :, 0:HD],
                                                rs.unsqueeze(3).broadcast_to([P, 4, HG, HD]),
                                                ALU.mult).then_inc(attn_ready, 1)
                    if group + 1 == NG and step < len(c_early) and c_early[step]:
                        early_c_job(*c_early[step])

            for tg in range(2, 4):
                residual(tg)
            normalise2(1)

            def add_output(tg):
                for pair in range(2):
                    dve.wait_ge(out_psum, tg * 2 + (pair + 1))
                    rows_of = x_sb[:, bass.ds(tg * 4 + 2 * pair, 2), :]
                    nc.vector.tensor_tensor(rows_of, psum[:, 6 + pair, :].rearrange("p (t d) -> p t d", d=D),
                                            rows_of, ALU.add).then_inc(out_ready, 1)

            def split_hidden(tg, last_output=False):
                for f in range(FC):
                    dve.wait_ge(hid_full_ready, tg * FC + (f + 1))
                    nc.vector.tensor_copy(hid_high[:, f, :], hid_full[:, f % HID_RING, :]).then_inc(hid_high_ready, 1)
                    dve.wait_ge(hid_high_ready, tg * FC + (f + 1))
                    nc.vector.tensor_tensor(hid_low[:, f, :], hid_full[:, f % HID_RING, :], hid_high[:, f, :],
                                            ALU.subtract).then_inc(hid_ready, 1)
                    if f == 3 and last_output:
                        add_output(tg - 1)

            split_hidden(0)
            for kind, tg, c in c_late:
                split_xn2(tg, c, c)
            with dve.Fori(1, TG) as tg:
                split_hidden(tg, last_output=True)
            add_output(TG - 1)


_INS = ["x", "cond_1024"] + ["L0_cond_" + n for n in (
    "ln1_w", "ln1_b", "ln2_w", "ln2_b", "wq", "bq", "wk", "bk", "wv", "bv", "wo", "bo",
    "wt_attn", "bt_attn", "wt_ffn", "bt_ffn", "w1", "b1", "w2", "b2")]


def kernel(**inputs):
    import numpy as np
    import concourse.bacc as bacc
    from concourse.bass_utils import run_bass_kernel_spmd

    nc = bacc.Bacc("TRN2", target_bir_lowering=False, num_devices=1)
    arrays, args = {}, []
    for name in _INS:
        a = np.ascontiguousarray(inputs[name])
        arrays["in_" + name] = a
        args.append(nc.dram_tensor("in_" + name, a.shape, mybir.dt.from_np(a.dtype), kind="ExternalInput").ap())
    args.append(nc.dram_tensor("out_dram", arrays["in_x"].shape, F32, kind="ExternalOutput").ap())
    layer_program(nc, *args)
    r = run_bass_kernel_spmd(nc, [arrays], core_ids=[0])
    return r.results[0]["out_dram"]
```

```python
from contextlib import ExitStack

import concourse.bass as bass
from concourse import mybir

F32 = mybir.dt.float32
F32R = mybir.dt.float32r
BF16 = mybir.dt.bfloat16
ACT = mybir.ActivationFunctionType
ALU = mybir.AluOpType
AX_X = mybir.AxisListType.X

P = 128
EPS = 1e-5
TERMS = [(0, 0), (0, 1), (1, 0), (0, 2), (2, 0), (1, 1)]

LN_W, LN_B, BQ, BK, BT, B1, COND, B2 = (0, 4), (2, 6), 8, 10, 12, 20, 28, 32
NCOLS = 34


def layer_program(nc, x, cond, ln1_w, ln1_b, ln2_w, ln2_b, wq, bq, wk, bk, wv, bv, wo, bo,
                  wt_attn, bt_attn, wt_ffn, bt_ffn, w1, b1, w2, b2, out):
    B, S, D = x.shape
    F = w1.shape[1]
    H = 16
    HD = D // H
    DC = D // P
    FC = F // P
    NT = B * S // P
    TB = S // P
    HG = 4
    NG = B * H // HG
    VW = HD + 1
    NTERM = len(TERMS)
    KS = NTERM * HD
    SLOTS = 3
    HS = S // 512
    STEPS = HS * TB
    TG = B * S // 512
    SCALE = float(HD) ** -0.5
    assert (D, F, S, B, HD) == (256, 1024, 1024, 2, 16)

    x_tiles = x.rearrange("b (t p) d -> p (b t) d", p=P)
    out_tiles = out.rearrange("b (t p) d -> p (b t) d", p=P)

    with ExitStack() as ctx:
        def sb(name, shape, dt):
            return ctx.enter_context(nc.sbuf_tensor(name, shape, dt))

        def sem(name):
            return ctx.enter_context(nc.semaphore(name))

        x_sb = sb("x_sb", [P, NT, D], F32)
        attn_sb = sb("attn_sb", [P, NG // 2, TB, 2, HG * HD], F32)
        v_group = sb("v_group", [P, TB, HG, 32], F32)
        wq_sb = sb("wq_sb", [P, DC, D], F32)
        wk_sb = sb("wk_sb", [P, DC, D], F32)
        wv_sb = sb("wv_sb", [P, DC, D], F32)
        wo_sb = sb("wo_sb", [P, DC, D], F32)
        w1_sb = sb("w1_sb", [P, DC, F], F32)
        w2_sb = sb("w2_sb", [P, FC, D], F32)
        rows = sb("rows", [NCOLS, P], F32)
        cols = sb("cols", [P, NCOLS], F32)
        bv_wide = sb("bv_wide", [P, B, H, VW], F32)
        bo_all = sb("bo_all", [P, D], F32)
        ident = sb("ident", [P, P], F32)
        ident_bf = sb("ident_bf", [P, P], BF16)
        t_mod = sb("t_mod", [P, 8, B], F32)
        mod_one = sb("mod_one", [P, 2, DC, B], F32)
        mod_mul = sb("mod_mul", [P, 2, DC, B], F32)
        mod_add = sb("mod_add", [P, 2, DC, B], F32)
        bn = sb("bn", [P, NT, 6], F32)
        mean_var = sb("mean_var", [P, NT, 2], F32)
        eps_col = sb("eps_col", [P, 1], F32)
        std = sb("std", [P, NT + 1], F32)
        rstd = sb("rstd", [P, NT], F32)
        rest = sb("rest", [P, 2, 512], F32)
        row_max = sb("row_max", [P, 2, TB], F32)
        neg_max = sb("neg_max", [P, 2, 2, TB], BF16)
        neg_max_t = sb("neg_max_t", [16, HG, P], BF16)
        rsum = sb("rsum", [P, 4 * HG], F32)

        with ExitStack() as first_use:
            def sb1(name, shape, dt):
                return first_use.enter_context(nc.sbuf_tensor(name, shape, dt))

            wt_sb = sb1("wt_sb", [P, 2, DC, 2 * D], F32)
            v_all = sb1("v_all", [P, NG, TB, HG * VW], F32)
            work = sb1("work", [P, 4096], F32)
            parts = sb1("parts", [P, 2 * 3, B * DC * S], BF16)
            stack = sb1("stack", [P, SLOTS * HG * 2, S], BF16)

        w1_low = sb("w1_low", [P, DC, F], F32R)
        w2_low = sb("w2_low", [P, FC, D], F32R)
        sb("unused_of_v_all", [P, 8 * D + NG * TB * HG * VW - 2 * DC * F], F32)
        HID_RING = 4
        hid_full = sb("hid_full", [P, HID_RING, 512], F32)
        mlp_out_t = sb("mlp_out_t", [P, DC, 512], F32)
        sb("unused_of_work", [P, 4096 - (HID_RING + DC) * 512], F32)
        w1_high = sb("w1_high", [P, DC, F], F32R)
        w2_high = sb("w2_high", [P, FC, D], F32R)
        attn_t = sb("attn_t", [P, 2, DC, 512], F32)
        xhat2 = sb("xhat2", [P, 2, 4, D], F32)
        xn2_high = sb("xn2_high", [P, DC, TG * 512], F32R)
        after_slot = {name: sb(name, [P, 8 * 512], F32R) for name in
                      sorted(("hid_high", "hid_low", "xn2_low"),
                             key=lambda n: (NG - 3 + ("xn2_low", "hid_high", "hid_low").index(n)) % SLOTS)}
        hid_high = after_slot["hid_high"][:, :].rearrange("p (f t) -> p f t", f=FC)
        hid_low = after_slot["hid_low"][:, :].rearrange("p (f t) -> p f t", f=FC)
        xn2_low = after_slot["xn2_low"][:, :].rearrange("p (c t) -> p c t", c=DC)

        out_t = rest[:, 0, :]
        xn_t = work[:, :].rearrange("p (c t) -> p c t", c=DC)
        probs = work[:, :].rearrange("p (a j q) -> p a j q", a=2, j=HG)
        xhat = attn_sb[:, :, :, :, :].rearrange("p n t o f -> p (n t o f)").rearrange("p (t d) -> p t d", d=D)
        attn_out = attn_sb[:, :, :, :, :]

        psum = ctx.enter_context(nc.psum_tensor("psum", [P, 8, 512], F32))
        ST_BANK, PV_BANK, MISC_BANK = 4, 6, 7

        rows_in = sem("rows_in")
        wt_in = [sem("wt_attn_in"), sem("wt_ffn_in")]
        x_in = [sem(f"x_in{tg}") for tg in range(TG)]
        wqk_in, wv_in, late_in = sem("wqk_in"), sem("wv_in"), sem("late_in")
        bv_wide_made, bv_in = sem("bv_wide_made"), sem("bv_in")
        ident_made, ones_made, v_ones_made = sem("ident_made"), sem("ones_made"), sem("v_ones_made")
        cols_psum, cols_ready = sem("cols_psum"), sem("cols_ready")
        mod_psum, mod_step = sem("mod_psum"), sem("mod_step")
        stats_step, var_ready, std_ready, rstd_ready = (
            sem("stats_step"), sem("var_ready"), sem("std_ready"), sem("rstd_ready"))
        xhat_ready, xn_ready = sem("xhat_ready"), sem("xn_ready")
        a_psum = sem("a_psum")
        high_ready, rest_ready, mid_ready, parts_ready = (
            sem("high_ready"), sem("rest_ready"), sem("mid_ready"), sem("parts_ready"))
        full_ready = sem("full_ready")
        v_ready = sem("v_ready")
        stack_in = [sem(f"stack_in{j}") for j in range(HG)]
        smax_psum, smax_read, neg_ready = sem("smax_psum"), sem("smax_read"), sem("neg_ready")
        row_max_done, neg_high = sem("row_max_done"), sem("neg_high")
        misc_psum = sem("misc_psum")
        neg_t_ready = sem("neg_t_ready")
        max_row_in = [sem(f"max_row_in{j}") for j in range(HG)]
        st_psum, probs_ready = sem("st_psum"), sem("probs_ready")
        pv_step = sem("pv_step")
        v_group_ready, out_t_ready = sem("v_group_ready"), sem("out_t_ready")
        rsum_ready, attn_ready = sem("rsum_ready"), sem("attn_ready")
        bo_added, w_high_made, w_split = sem("bo_added"), sem("w_high_made"), sem("w_split")
        c_psum = sem("c_psum")
        attn_t_ready, x1_ready = sem("attn_t_ready"), sem("x1_ready")
        stats2_step, var2_ready, std2_ready, rstd2_ready = (
            sem("stats2_step"), sem("var2_ready"), sem("std2_ready"), sem("rstd2_ready"))
        xhat2_ready, xn2_full_ready, xn2_high_ready, xn2_ready = (
            sem("xhat2_ready"), sem("xn2_full_ready"), sem("xn2_high_ready"), sem("xn2_ready"))
        hid_psum, hid_full_ready, hid_high_ready, hid_ready = (
            sem("hid_psum"), sem("hid_full_ready"), sem("hid_high_ready"), sem("hid_ready"))
        mlp_out_psum, mlp_out_t_ready = sem("mlp_out_psum"), sem("mlp_out_t_ready")
        out_psum, out_ready, out_stored = sem("out_psum"), sem("out_ready"), sem("out_stored")

        a_jobs = []
        for b in range(B):
            tgs = range(b * TG // B, (b + 1) * TG // B)
            a_jobs += [("T", b, tg, c) for tg in tgs for c in range(DC)]
            for c in range(DC):
                a_jobs += [(kind, b, tg, c) for tg in tgs for kind in "QK"]
            a_jobs += [("V", b, tg, pair) for tg in tgs for pair in range(2)]
        EARLY = (HG + 1) * TB - 2
        A_RING = 3

        JOBS_BEFORE = 11
        JOB_COST = {"T": 1, "Q": 4, "K": 4, "V": 4}

        def tiles_by(i):
            def cost(jobs):
                return sum(JOB_COST[job[0]] for job in jobs[JOBS_BEFORE:])
            return EARLY * cost(a_jobs[:i]) // cost(a_jobs[:-1])

        def early_tiles(i):
            return range(tiles_by(max(i - 1, 0)), tiles_by(i))

        a_index = {job: i for i, job in enumerate(a_jobs)}
        qk_jobs = [job for job in a_jobs if job[0] in "QK"]

        def jobs(*names):
            return [(name[0], int(name[1]), c) for name in names for c in range(2)]

        A_OF_GROUP_6 = [("A", 2, 0), ("A", 3, 0)]
        c_early = {0: jobs("A0"), 1: jobs("A1"), 2: [("O", 0, 0)], 3: [("O", 0, 1)], 4: [("O", 1, 0)],
                   5: [("O", 1, 1)], 7: A_OF_GROUP_6, 9: [("T", 0, 0)], 10: [("T", 0, 1)],
                   11: [("T", 1, 0)], 12: [("T", 1, 1)]}
        DEV2_STEP = 7
        HIDDEN_STEPS = {13: 0, 14: 1}
        c_middle_a, c_middle_o, c_late = [("A", 2, 1), ("A", 3, 1)], jobs("O2", "O3"), jobs("T2", "T3")
        c_order = [job for step in c_early for job in c_early[step]] + c_middle_a + c_middle_o + c_late
        c_index = {job: i for i, job in enumerate(c_order)}

        def c_bank(kind, tg, c):
            if (kind, tg, c) in A_OF_GROUP_6:
                return tg % 2
            if tg < 2:
                return c
            return (6 if kind == "T" or tg == 3 else 4) + c

        LAST_MAX_STEP = (NG - 1) * STEPS - 4

        def st_bank(tile):
            return (4, 5, 2, 3)[tile % HG] if tile // HG > LAST_MAX_STEP else ST_BANK + tile % 2

        def a_read(i):
            kind, b, tg, c = a_jobs[i]
            if kind == "T":
                return xn_ready, DC * tg + c + 1
            if kind == "V":
                return v_ready, 2 * (2 * tg + c + 1)
            return high_ready if b else rest_ready, qk_jobs.index(a_jobs[i]) + 1

        def c_read(kind, tg, c):
            done = {"A": attn_t_ready, "O": x1_ready, "T": xn2_full_ready}[kind]
            return done, [x for x in c_order if x[0] == kind].index((kind, tg, c)) + 1

        def c_before(job):
            return [x for x in c_order[:c_order.index(job)] if c_bank(*x) == c_bank(*job)][-1:]

        def token_slice(b, c, tg):
            at = (b * DC + c) * S + (tg % (TG // B)) * 512
            return slice(at, at + 512)

        def head_in_stack(slot, j, side, first, size):
            return bass.ds(slot + ((2 * j + side) * S + first), size)

        def slot_of(group):
            return (group % SLOTS) * (HG * 2 * S)

        def misc_use(group, j):
            return j + 1 if group == 0 else HG + 6 * (group - 1) + j + 1 + (j >= 2)

        stack_flat = stack[:, :, :].rearrange("p a t -> p (a t)")
        parts_flat = parts[:, :, :]

        def load_x(engine, tg):
            tiles = slice(4 * tg, 4 * tg + 4)
            engine.dma_start(x_sb[:, tiles, :], x_tiles[:, tiles, :]).then_inc(x_in[tg], 16)

        block = ctx.enter_context(nc.Block())

        @block.sync
        def _(sp):
            for at, vec in ((0, ln1_w), (2, ln1_b), (4, ln2_w), (6, ln2_b), (8, bq), (10, bk), (12, bt_attn)):
                r = vec.rearrange("(r k) -> r k", k=P)
                sp.dma_start(rows[at:at + r.shape[0], :], r).then_inc(rows_in, 16)
            load_x(sp, 2)
            load_x(sp, 3)
            sp.dma_start(wv_sb[:, :, :], wv.rearrange("(c k) n -> k c n", k=P)).then_inc(wv_in, 16)
            sp.wait_ge(bv_wide_made, 1)
            for b in range(B):
                sp.dma_start(bv_wide[:, b, :, 0:HD], bv.rearrange("(h d) -> h d", d=HD).partition_broadcast(P)).then_inc(bv_in, 16)
            for dst, src in ((wo_sb, wo), (w1_sb, w1), (w2_sb, w2)):
                sp.dma_start(dst[:, :, :], src.rearrange("(c k) n -> k c n", k=P)).then_inc(late_in, 16)
            for dst, src in ((bo_all, bo),):
                sp.dma_start(dst[:, :], src.partition_broadcast(P)).then_inc(late_in, 16)

            def load_head(group, pair, odd, j):
                p0 = 64 * odd + 16 * j
                slot = (group % SLOTS) * (HG * 2)
                for t, (a, b) in enumerate(TERMS):
                    src = parts_flat[p0:p0 + HD, a:4 + b:3 + b - a, bass.ds(pair * S, S)]
                    at = slot + 2 * j
                    sp.dma_start(stack[t * HD:(t + 1) * HD, bass.ds(at, 2), :], src).then_inc(stack_in[j], 16)

            def store_max(group, j):
                slot = slot_of(group)
                sp.wait_ge(neg_t_ready, 4 * group + j + 1)
                for part in range(2):
                    sp.dma_start(stack_flat[KS + part:KS + part + 1, head_in_stack(slot, j, 0, 0, S)],
                                 neg_max_t[part * TB:(part + 1) * TB, j, :]).then_inc(max_row_in[j], 16)

            sp.wait_ge(parts_ready, 4)
            for j in range(HG):
                load_head(0, 0, 0, j)
            for j in range(HG):
                sp.wait_ge(stack_in[j], 16 * NTERM)
                load_head(1, 0, 1, j)
                store_max(0, j)
            sp.wait_ge(parts_ready, len(qk_jobs))
            for group in range(2, NG):
                sp.wait_ge(st_psum, (group - 2) * (STEPS * HG) + 1)
                for j in range(HG):
                    sp.wait_ge(stack_in[j], 16 * NTERM * group)
                    load_head(group, group // 2, group % 2, j)
                    store_max(group - 1, j)
            for j in range(HG):
                store_max(NG - 1, j)
            with sp.Fori(0, TG) as tg:
                for pair in range(2):
                    sp.wait_ge(out_ready, 2 + tg * 2 + (pair + 1))
                    sp.dma_start(out_tiles[:, bass.ds(tg * 4 + 2 * pair, 2), :],
                                 x_sb[:, bass.ds(tg * 4 + 2 * pair, 2), :]).then_inc(out_stored, 16)
            sp.wait_ge(out_stored, 16 * 2 * TG)

        @block.gpsimd
        def _(pool):
            nc.gpsimd.memset(ident[:, :], 0.0).then_inc(ident_made, 1)
            pool.wait_ge(ident_made, 1)
            nc.gpsimd.affine_select(out=ident[:, :], in_=ident[:, :], compare_op=ALU.not_equal, fill=1.0,
                                    base=0, pattern=[[-1, P]], channel_multiplier=1).then_inc(ident_made, 1)
            pool.wait_ge(ident_made, 2)
            nc.gpsimd.tensor_copy(ident_bf[:, :], ident[:, :]).then_inc(ident_made, 1)
            nc.gpsimd.memset(bv_wide[:, :, :, :], 0.0).then_inc(bv_wide_made, 1)
            nc.gpsimd.memset(v_all[:, :, :, :], 1.0).then_inc(v_ones_made, 1)
            nc.gpsimd.memset(v_group[:, :, :, :], 0.0).then_inc(v_ones_made, 1)
            pool.wait_ge(v_ones_made, 2)
            for s in range(SLOTS):
                sides = stack[KS:P, s * HG * 2:(s + 1) * HG * 2, :]
                nc.gpsimd.memset(sides[:, 1::2, :], 1.0).then_inc(ones_made, 1)
            pool.wait_ge(ones_made, SLOTS)
            def low_part(i):
                kind, b, tg, c = qk_jobs[i]
                side = 3 * (kind == "K")
                pool.wait_ge(mid_ready, i + 1)
                nc.gpsimd.tensor_tensor(parts[:, side + 2, token_slice(b, c, tg)], rest[:, i % 2, :],
                                        parts[:, side + 1, token_slice(b, c, tg)],
                                        ALU.subtract).then_inc(parts_ready, 1)

            def rest_part(i):
                kind, b, tg, c = qk_jobs[i]
                pool.wait_ge(full_ready, i - len(qk_jobs) // B + 1)
                pool.wait_ge(high_ready, i + 1)
                nc.gpsimd.tensor_tensor(rest[:, i % 2, :], rest[:, i % 2, :],
                                        parts[:, 3 * (kind == "K"), token_slice(b, c, tg)],
                                        ALU.subtract).then_inc(rest_ready, 1)

            first_of_1 = len(qk_jobs) // B
            for i in range(first_of_1):
                low_part(i)
            for i in range(first_of_1, len(qk_jobs)):
                rest_part(i)
                if i > first_of_1:
                    low_part(i - 1)
            low_part(len(qk_jobs) - 1)

            bv_groups = bv_wide[:, :, :, :].rearrange("p b h w -> p (b h w)").rearrange("p (n w) -> p n w", n=NG)

            def fill_v(group, half):
                chunks = slice(half * 4, half * 4 + 4)
                nc.gpsimd.tensor_tensor(
                    v_group[:, chunks, :, 0:VW],
                    v_all[:, bass.ds(group, 1), chunks, :].rearrange("p n k (j w) -> p (n k) j w", j=HG),
                    bv_groups[:, bass.ds(group, 1), :].rearrange("p n (j w) -> p n j w", j=HG).broadcast_to([P, 4, HG, VW]),
                    ALU.add).then_inc(v_group_ready, 1)

            pool.wait_ge(v_ready, 8)
            pool.wait_ge(bv_in, 16 * B)
            pool.wait_ge(v_ones_made, 2)
            for half in range(2):
                fill_v(0, half)
            pool.wait_ge(late_in, 16 * 4)
            for t in range(NT):
                nc.gpsimd.tensor_tensor(x_sb[:, t, :], x_sb[:, t, :], bo_all[:, :], ALU.add).then_inc(bo_added, 1)
            def refill_v(group):
                for half in range(2):
                    pool.wait_ge(pv_step, group * STEPS - (4 - 4 * half))
                    fill_v(group, half)

            with pool.Fori(1, NG - 1) as group:
                refill_v(group)
            for j in range(HG):
                pool.wait_ge(stack_in[j], 16 * NTERM * NG)
            def split_weight(i, high, low, w):
                nc.gpsimd.tensor_copy(high[:, :, :], w[:, :, :]).then_inc(w_high_made, 1)
                pool.wait_ge(w_high_made, i + 1)
                nc.gpsimd.tensor_tensor(low[:, :, :], w[:, :, :], high[:, :, :], ALU.subtract).then_inc(w_split, 1)

            split_weight(0, w1_high, w1_low, w1_sb)
            refill_v(NG - 1)
            pool.wait_ge(v_group_ready, 2 * NG)
            split_weight(1, w2_high, w2_low, w2_sb)

        @block.tensor
        def _(pe):
            pe.wait_ge(ident_made, 2)
            pe.wait_ge(rows_in, 16 * 11)
            nc.tensor.transpose(psum[:, 0, 0:NCOLS], rows[:, :], ident[0:NCOLS, 0:NCOLS]).then_inc(cols_psum, 1)
            pe.wait_ge(cols_ready, 1)

            def modulation(which):
                pe.wait_ge(wt_in[which], 16)
                for f in range(4):
                    for c in range(DC):
                        last = nc.tensor.matmul(psum[:, 1 + which, f * B:(f + 1) * B],
                                                wt_sb[:, which, c, f * P:(f + 1) * P],
                                                cols[:, COND + c:COND + c + 3:2],
                                                start=(c == 0), stop=(c == DC - 1))
                last.then_inc(mod_psum, 1)

            modulation(0)

            def scores_for_max(tile, slot, j, qc, half):
                if half == 0 and tile >= 2:
                    pe.wait_ge(smax_read, tile - 1)
                last = nc.tensor.matmul(
                    psum[:, 2 * (qc % 2) + half, :],
                    stack_flat[0:KS, head_in_stack(slot, j, 0, qc * P, P)],
                    stack_flat[0:KS, head_in_stack(slot, j, 1, half * 512, 512)],
                    start=True, stop=True)
                if half == 1:
                    last.then_inc(smax_psum, 1)

            def turn_max(head, j):
                if head:
                    pe.wait_ge(neg_t_ready, head)
                pe.wait_ge(neg_ready, head + 1)
                nc.tensor.transpose(psum[0:16, MISC_BANK, 0:64].bitcast(BF16),
                                    neg_max[:, j % 2, :, :].rearrange("p a t -> p (a t)"),
                                    ident_bf[:, :]).then_inc(misc_psum, 1)

            def scores_for_exp(slot, step, j, tile):
                half, kc = divmod(step, TB)
                same = [u for u in range(max(tile - HG, 0), tile) if st_bank(u) == st_bank(tile)]
                if same:
                    pe.wait_ge(probs_ready, same[-1] + 1)
                elif tile > HG:
                    pe.wait_ge(smax_read, NG * HG * TB)
                last = nc.tensor.matmul(
                    psum[:, st_bank(tile), :],
                    stack_flat[0:KS + 2, head_in_stack(slot, j, 1, kc * P, P)],
                    stack_flat[0:KS + 2, head_in_stack(slot, j, 0, half * 512, 512)],
                    start=True, stop=True)
                last.then_inc(st_psum, 1)
                return last

            def first_maxima(tile):
                head, qc = divmod(tile, TB)
                if qc == 0:
                    pe.wait_ge(stack_in[head % HG], 16 * NTERM * (head // HG + 1))
                for half in range(2):
                    scores_for_max(tile, slot_of(head // HG), head % HG, qc, half)
                if qc == 3 and head:
                    turn_max(head - 1, head - 1)

            pe.wait_ge(ident_made, 3)
            for i, (kind, b, tg, c) in enumerate(a_jobs):
                for tile in early_tiles(i):
                    if tile == 0:
                        modulation(1)
                        pe.wait_ge(mod_step, 10)
                    first_maxima(tile)
                bank = 4 + i % A_RING
                if i >= A_RING:
                    pe.wait_ge(*a_read(i - A_RING))
                if kind == "T":
                    pe.wait_ge(xhat_ready, 4 * tg + 4)
                    for t in range(4):
                        last = nc.tensor.transpose(psum[:, bank, t * P:(t + 1) * P],
                                                   xhat[:, 4 * tg + t, c * P:(c + 1) * P], ident[:, :])
                    last.then_inc(a_psum, 1)
                    continue
                pe.wait_ge(xn_ready, DC * (tg + 1))
                if kind in "QK":
                    pe.wait_ge(wqk_in, 32)
                    w = wq_sb if kind == "Q" else wk_sb
                    for k in range(DC):
                        last = nc.tensor.matmul(psum[:, bank, :], w[:, k, c * P:(c + 1) * P],
                                                xn_t[:, k, tg * 512:(tg + 1) * 512],
                                                start=(k == 0), stop=(k == DC - 1))
                else:
                    pe.wait_ge(wv_in, 16)
                    for t in range(2):
                        token = (4 * tg + 2 * c + t) * P
                        for k in range(DC):
                            last = nc.tensor.matmul(psum[:, bank, t * D:(t + 1) * D],
                                                    xn_t[:, k, token:token + P], wv_sb[:, k, :],
                                                    start=(k == 0), stop=(k == DC - 1))
                last.then_inc(a_psum, 1)

            late_tiles = range(early_tiles(len(a_jobs) - 1).stop, (HG + 1) * TB)
            for i in range(len(a_jobs) - A_RING, len(a_jobs)):
                pe.wait_ge(*a_read(i))
            pe.wait_ge(ones_made, SLOTS)
            for j in range(HG):
                pe.wait_ge(max_row_in[j], 32)
                scores_for_exp(0, 0, j, j)
                if j % 2:
                    for tile in late_tiles[j // 2::2]:
                        first_maxima(tile)

            def c_job(kind, tg, c):
                bank = c_bank(kind, tg, c)
                for job in c_before((kind, tg, c)):
                    pe.wait_ge(*c_read(*job))
                if kind == "A":
                    for t in range(4):
                        b, tb = divmod(4 * tg + t, TB)
                        last = nc.tensor.transpose(
                            psum[:, bank, t * P:(t + 1) * P],
                            attn_out[:, b * DC + c, tb, :, :].rearrange("p o f -> p (o f)"), ident[:, :])
                elif kind == "O":
                    pe.wait_ge(*c_read("A", tg, DC - 1))
                    for t in range(2):
                        at = (2 * c + t) * P
                        for k in range(DC):
                            last = nc.tensor.matmul(psum[:, bank, t * D:(t + 1) * D],
                                                    attn_t[:, tg % 2, k, at:at + P], wo_sb[:, k, :],
                                                    start=(k == 0), stop=(k == DC - 1))
                else:
                    pe.wait_ge(xhat2_ready, 4 * (tg + 1))
                    for t in range(4):
                        last = nc.tensor.transpose(psum[:, bank, t * P:(t + 1) * P],
                                                   xhat2[:, tg % 2, t, c * P:(c + 1) * P], ident[:, :])
                last.then_inc(c_psum, 1)

            def three_products(out, w, x, first, last):
                for i, (a, b) in enumerate(((0, 0), (0, 1), (1, 0))):
                    mm = nc.tensor.matmul(out, w[a], x[b], start=first and i == 0, stop=last and i == 2)
                return mm

            def hidden_chunk(tg, f):
                if f >= 4:
                    pe.wait_ge(hid_full_ready, tg * FC + (f - 3))
                tokens, hidden = bass.ds(tg * 512, 512), slice(f * P, (f + 1) * P)
                for k in range(DC):
                    last = three_products(psum[:, f % 4, :], (w1_high[:, k, hidden], w1_low[:, k, hidden]),
                                          (xn2_high[:, k, tokens], xn2_low[:, k, tokens]),
                                          k == 0, k == DC - 1)
                last.then_inc(hid_psum, 1)

            def mlp_output(tg, jobs_between=()):
                for f in range(FC):
                    if f == 2:
                        for job in jobs_between:
                            c_job(*job)
                    pe.wait_ge(hid_ready, tg * FC + (f + 1))
                    for c in range(DC):
                        feats = slice(c * P, (c + 1) * P)
                        last = three_products(psum[:, 4 + c, :], (w2_high[:, f, feats], w2_low[:, f, feats]),
                                              (hid_high[:, f, :], hid_low[:, f, :]), f == 0, f == FC - 1)
                        if f == FC - 1:
                            last.then_inc(mlp_out_psum, 1)

            def mlp_back(tg):
                pe.wait_ge(mlp_out_t_ready, (tg + 1) * DC)
                for pair in range(2):
                    pe.wait_ge(out_ready, tg * 2 + (pair + 1))
                    for t in range(2):
                        for c in range(DC):
                            at = (2 * pair + t) * P
                            last = nc.tensor.transpose(psum[:, 6 + pair, t * D + c * P:t * D + (c + 1) * P],
                                                       mlp_out_t[:, c, at:at + P], ident[:, :])
                    last.then_inc(out_psum, 1)

            def group_steps(group):
                more = group + 1 < NG
                slot, next_slot = slot_of(group), slot_of(group + 1)
                for step in range(STEPS):
                    ahead = (group + 1) * HG + 1 + step // 4
                    ahead_group, ahead_j = divmod(ahead, HG)
                    qc = (2 * step) % TB
                    last_of_group = step + 1 == STEPS

                    def next_scores(j):
                        if last_of_group and not more:
                            return
                        if last_of_group:
                            pe.wait_ge(max_row_in[j], 32 * (group + 2))
                        scores_for_exp(next_slot if last_of_group else slot, (step + 1) % STEPS, j,
                                       (group * STEPS + step + 1) * HG + j)

                    def max_scores(tile, half):
                        if ahead < NG * HG:
                            scores_for_max(ahead * TB + qc + tile, slot_of(ahead_group), ahead_j, qc + tile, half)

                    if step % 4 == 0 and ahead < NG * HG:
                        pe.wait_ge(stack_in[ahead_j], 16 * NTERM * (ahead_group + 1))
                    max_scores(0, 0)
                    next_scores(0)
                    max_scores(0, 1)
                    next_scores(1)
                    pe.wait_ge(probs_ready, (group * STEPS + step + 1) * HG)
                    if step == 0 or step == 4:
                        pe.wait_ge(v_group_ready, group * 2 + 1 + step // 4)
                    if step % TB == 0 and (group or step):
                        pe.wait_ge(out_t_ready, group * 2 + step // TB)
                    for j in range(HG):
                        last = nc.tensor.matmul(psum[32 * j:32 * j + 32, PV_BANK, :],
                                                v_group[:, step % TB, j, :], probs[:, step % 2, j, :],
                                                start=(step % TB == 0), stop=(step % TB == TB - 1))
                    last.then_inc(pv_step, 1)
                    next_scores(2)
                    max_scores(1, 0)
                    next_scores(3)
                    max_scores(1, 1)
                    if step % 4 == 0 and more:
                        if step % TB == 0 and (group or step):
                            pe.wait_ge(attn_ready, group * 2 + step // TB)
                        turn_max((group + 1) * HG + step // 4, step // 4)
                    if step % TB == TB - 1:
                        half = step // TB
                        if more:
                            pe.wait_ge(neg_t_ready, (group + 1) * HG + 2 * half + 2)
                        else:
                            pe.wait_ge(attn_ready, group * 2 + half)
                        if last_of_group and not more:
                            pe.wait_ge(probs_ready, NG * STEPS * HG)
                            hidden_chunk(0, 2)
                        pe.wait_ge(out_t_ready, group * 2 + half + 1)
                        for t in range(4):
                            last = nc.tensor.transpose(psum[:, MISC_BANK, t * P:(t + 1) * P],
                                                       out_t[:, t * P:(t + 1) * P], ident[:, :])
                        last.then_inc(misc_psum, 1)
                    if more:
                        continue
                    if step == 0:
                        pe.wait_ge(smax_read, NG * HG * TB)
                        pe.wait_ge(attn_ready, NG)
                        pe.wait_ge(late_in, 16 * 4)
                    for job in c_early.get(step, ()):
                        if job in A_OF_GROUP_6:
                            pe.wait_ge(attn_ready, 2 * (NG - 1))
                        c_job(*job)
                    if step in HIDDEN_STEPS:
                        pe.wait_ge(xn2_ready, DC * 2)
                        pe.wait_ge(w_split, 2)
                        pe.wait_ge(*c_read("T", 1, HIDDEN_STEPS[step]))
                        hidden_chunk(0, HIDDEN_STEPS[step])

            for group in range(NG):
                group_steps(group)

            hidden_chunk(0, 3)
            pe.wait_ge(attn_ready, 2 * NG)
            for job in c_middle_a + c_middle_o[:2]:
                c_job(*job)
            hidden_chunk(0, 4)
            for job in c_middle_o[2:]:
                c_job(*job)
            for f in range(5, FC):
                hidden_chunk(0, f)
            pe.wait_ge(x1_ready, 2 * 3)
            mlp_output(0, c_late)
            pe.wait_ge(xn2_ready, DC * TG)
            with pe.Fori(1, TG) as tg:
                for f in range(FC):
                    hidden_chunk(tg, f)
                    if f == 1:
                        mlp_back(tg - 1)
                pe.wait_ge(mlp_out_t_ready, tg * DC)
                mlp_output(tg)
            mlp_back(TG - 1)

        @block.scalar
        def _(act):
            load_x(act, 0)
            load_x(act, 1)
            for at, vec in ((16, bt_ffn), (20, b1), (32, b2)):
                r = vec.rearrange("(r k) -> r k", k=P)
                act.dma_start(rows[at:at + r.shape[0], :], r).then_inc(rows_in, 16)
            act.dma_start(rows[28:32, :], cond.rearrange("b (c k) -> (b c) k", k=P)).then_inc(rows_in, 16)
            for which, w in enumerate((wt_attn, wt_ffn)):
                act.dma_start(wt_sb[:, which, :, :], w.rearrange("(c k) n -> k c n", k=P)).then_inc(wt_in[which], 16)
            for dst, src in ((wq_sb, wq), (wk_sb, wk)):
                act.dma_start(dst[:, :, :], src.rearrange("(c k) n -> k c n", k=P)).then_inc(wqk_in, 16)

            def deviation(tg):
                act.wait_ge(var_ready, tg + 1)
                nc.scalar.activation(std[:, 4 * tg:4 * tg + 4], mean_var[:, 4 * tg:4 * tg + 4, 1],
                                     ACT.Sqrt, bias=eps_col[:, 0:1]).then_inc(std_ready, 1)

            def xn_out(tg, c, b):
                i = a_index[("T", b, tg, c)]
                act.wait_ge(a_psum, i + 1)
                nc.scalar.activation(xn_t[:, c, tg * 512:(tg + 1) * 512], psum[:, 4 + i % A_RING, :], ACT.Identity,
                                     bias=mod_add[:, 0, c, b:b + 1],
                                     scale=mod_mul[:, 0, c, b:b + 1]).then_inc(xn_ready, 1)

            def high_part(i):
                kind, b, tg, c = qk_jobs[i]
                at = a_index[qk_jobs[i]]
                act.wait_ge(a_psum, at + 1)
                col = (BQ if kind == "Q" else BK) + c
                if b:
                    act.wait_ge(parts_ready, i - 1)
                    nc.scalar.activation(rest[:, i % 2, :], psum[:, 4 + at % A_RING, :],
                                         ACT.Identity, bias=cols[:, col:col + 1]).then_inc(full_ready, 1)
                nc.scalar.activation(parts[:, 3 * (kind == "K"), token_slice(b, c, tg)], psum[:, 4 + at % A_RING, :],
                                     ACT.Identity, bias=cols[:, col:col + 1]).then_inc(high_ready, 1)

            def middle_part(i):
                kind, b, tg, c = qk_jobs[i]
                act.wait_ge(rest_ready, i + 1)
                nc.scalar.copy(parts[:, 3 * (kind == "K") + 1, token_slice(b, c, tg)],
                               rest[:, i % 2, :]).then_inc(mid_ready, 1)

            def v_out(b, tg, pair):
                at = a_index[("V", b, tg, pair)]
                act.wait_ge(a_psum, at + 1)
                if b == 0:
                    act.wait_ge(v_ones_made, 1)
                for t in range(2):
                    kc = (4 * tg + 2 * pair + t) % TB
                    dst = v_all[:, b * HG:(b + 1) * HG, kc, :].rearrange("p g (j w) -> p g j w", j=HG)
                    nc.scalar.copy(
                        dst[:, :, :, 0:HD],
                        psum[:, 4 + at % A_RING, t * D:(t + 1) * D].rearrange("p (g j d) -> p g j d", g=HG, j=HG)
                    ).then_inc(v_ready, 1)

            def turned_max(group, j):
                act.wait_ge(misc_psum, misc_use(group, j))
                if group:
                    act.wait_ge(max_row_in[j], 32 * group)
                nc.scalar.copy(neg_max_t[:, j, :], psum[0:16, MISC_BANK, 0:64].bitcast(BF16)).then_inc(neg_t_ready, 1)

            def first_turned(tile):
                if tile % TB == 3 and tile > TB:
                    turned_max(0, tile // TB - 1)

            deviation(0)
            deviation(1)
            act.wait_ge(mod_step, 5)
            for i, (kind, b, tg, c) in enumerate(a_jobs):
                for tile in early_tiles(i):
                    first_turned(tile)
                if kind == "T":
                    xn_out(tg, c, b)
                    if i == 3:
                        deviation(2)
                        deviation(3)
                if kind in "QK":
                    n = qk_jobs.index(a_jobs[i])
                    high_part(n)
                    if n % (len(qk_jobs) // B):
                        middle_part(n - 1)
                if kind == "V" and tg % (TG // B) == 0 and c == 0:
                    middle_part((b + 1) * len(qk_jobs) // B - 1)
                    if b:
                        nc.scalar.activation(std[:, NT:NT + 1], eps_col[:, 0:1], ACT.Exp)
                if kind == "V":
                    v_out(b, tg, c)
            for tile in range(early_tiles(len(a_jobs) - 1).stop, (HG + 1) * TB):
                first_turned(tile)

            def exponentials(tile):
                act.wait_ge(st_psum, tile + 1)
                nc.scalar.activation(probs[:, tile // HG % 2, tile % HG, :], psum[:, st_bank(tile), :], ACT.Exp,
                                     scale=SCALE).then_inc(probs_ready, 1)

            act.wait_ge(a_psum, len(a_jobs))
            def deviation2(b):
                act.wait_ge(var2_ready, 2 * b + 2)
                nc.scalar.activation(std[:, b * TB:(b + 1) * TB], mean_var[:, b * TB:(b + 1) * TB, 1],
                                     ACT.Sqrt, bias=eps_col[:, 0:1]).then_inc(std2_ready, 1)

            for j in range(HG):
                exponentials(j)
            for group in range(NG):
                more = group + 1 < NG
                for step in range(STEPS):
                    for j in range(HG):
                        if step + 1 < STEPS or more:
                            if j == 0 and (group or step):
                                act.wait_ge(pv_step, group * STEPS + step)
                            exponentials((group * STEPS + step + 1) * HG + j)
                        if j == 1 and step % 4 == 1 and more:
                            turned_max(group + 1, step // 4)
                        if j == 1 and step == DEV2_STEP and not more:
                            deviation2(0)
                        if step % TB == TB - 1 and j == 1:
                            half = step // TB
                            act.wait_ge(pv_step, group * STEPS + step + 1)
                            if group or half:
                                act.wait_ge(attn_ready, group * 2 + half)
                            nc.scalar.copy(out_t, psum[:, PV_BANK, :]).then_inc(out_t_ready, 1)

            def c_job(kind, tg, c):
                act.wait_ge(c_psum, c_index[kind, tg, c] + 1)
                src = psum[:, c_bank(kind, tg, c), :]
                if kind == "A":
                    nc.scalar.copy(attn_t[:, tg % 2, c, :], src).then_inc(attn_t_ready, 1)
                else:
                    act.wait_ge(xn2_ready, DC * tg + c - 1)
                    b = tg * B // TG
                    nc.scalar.activation(rest[:, c, :], src, ACT.Identity,
                                         bias=mod_add[:, 1, c, b:b + 1],
                                         scale=mod_mul[:, 1, c, b:b + 1]).then_inc(xn2_full_ready, 1)

            def hidden(tg, first=False, chunks=range(FC)):
                for f in chunks:
                    act.wait_ge(hid_psum, tg * FC + (f + 1))
                    if f >= HID_RING or not first:
                        act.wait_ge(hid_ready, tg * FC + (f + 1 - HID_RING))
                    nc.scalar.activation(hid_full[:, f % HID_RING, :], psum[:, f % 4, :], ACT.Gelu,
                                         bias=cols[:, B1 + f:B1 + f + 1]).then_inc(hid_full_ready, 1)

            def output(tg, first=False):
                for c in range(DC):
                    act.wait_ge(mlp_out_psum, tg * DC + (c + 1))
                    if c == 0 and not first:
                        act.wait_ge(out_psum, tg * 2)
                    nc.scalar.activation(mlp_out_t[:, c, :], psum[:, 4 + c, :], ACT.Identity,
                                         bias=cols[:, B2 + c:B2 + c + 1]).then_inc(mlp_out_t_ready, 1)

            hidden(0, True, range(0, 2))
            for job in c_middle_a:
                c_job(*job)
            hidden(0, True, range(2, 4))
            deviation2(1)
            hidden(0, True, range(4, FC))
            for job in c_late:
                c_job(*job)
            output(0, first=True)
            with act.Fori(1, TG) as tg:
                hidden(tg)
                output(tg)

        @block.vector
        def _(dve):
            nc.vector.memset(eps_col[:, :], EPS).then_inc(stats_step, 1)
            nc.vector.memset(rsum[:, :], 0.0).then_inc(out_ready, 2)

            def stats(tg):
                dve.wait_ge(x_in[tg], 16)
                for t in range(4 * tg, 4 * tg + 4):
                    nc.vector.bn_stats(bn[:, t, :], x_sb[:, t, :]).then_inc(stats_step, 1)
                dve.wait_ge(stats_step, 1 + 4 * (tg + 1))
                for t in range(4 * tg, 4 * tg + 4):
                    last = nc.vector.bn_aggr(mean_var[:, t, :], bn[:, t, :])
                last.then_inc(var_ready, 1)

            def normalise(tg):
                dve.wait_ge(std_ready, tg + 1)
                tiles = slice(4 * tg, 4 * tg + 4)
                nc.vector.reciprocal(rstd[:, tiles], std[:, tiles]).then_inc(rstd_ready, 1)
                dve.wait_ge(rstd_ready, tg + 1)
                for t in range(4 * tg, 4 * tg + 4):
                    nc.vector.tensor_scalar(xhat[:, t, :], x_sb[:, t, :], mean_var[:, t, 0:1],
                                            rstd[:, t:t + 1], ALU.subtract, ALU.mult).then_inc(xhat_ready, 1)

            t_mod_v = t_mod[:, :, :].rearrange("p (l s c) b -> p l s c b", l=2, s=2)

            def modulation(l):
                done = 5 * l
                dve.wait_ge(mod_psum, l + 1)
                nc.vector.tensor_tensor(t_mod[:, 4 * l:4 * l + 4, :],
                                        psum[:, 1 + l, 0:4 * B].rearrange("p (f b) -> p f b", b=B),
                                        cols[:, BT + 4 * l:BT + 4 * l + 4].unsqueeze(2).broadcast_to([P, 4, B]),
                                        ALU.add).then_inc(mod_step, 1)
                dve.wait_ge(mod_step, done + 1)
                nc.vector.tensor_scalar(mod_one[:, l, :, :], t_mod_v[:, l, 1, :, :], 1.0, None,
                                        ALU.add).then_inc(mod_step, 1)
                dve.wait_ge(mod_step, done + 2)
                for dst, at in ((mod_mul, LN_W[l]), (mod_add, LN_B[l])):
                    nc.vector.tensor_tensor(dst[:, l, :, :], mod_one[:, l, :, :],
                                            cols[:, at:at + DC].unsqueeze(2).broadcast_to([P, DC, B]),
                                            ALU.mult).then_inc(mod_step, 1)
                dve.wait_ge(mod_step, done + 4)
                nc.vector.tensor_tensor(mod_add[:, l, :, :], mod_add[:, l, :, :], t_mod_v[:, l, 0, :, :],
                                        ALU.add).then_inc(mod_step, 1)

            stats(0)
            dve.wait_ge(cols_psum, 1)
            nc.vector.tensor_copy(cols[:, :], psum[:, 0, 0:NCOLS]).then_inc(cols_ready, 1)
            stats(1)
            normalise(0)
            dve.wait_ge(cols_ready, 1)
            modulation(0)
            normalise(1)
            stats(2)
            stats(3)
            normalise(2)
            normalise(3)

            def rest_part(i):
                kind, b, tg, c = qk_jobs[i]
                at = a_index[qk_jobs[i]]
                dve.wait_ge(high_ready, i + 1)
                if i >= 2:
                    dve.wait_ge(parts_ready, i - 1)
                col = (BQ if kind == "Q" else BK) + c
                nc.vector.scalar_tensor_tensor(
                    out=rest[:, i % 2, :], in0=psum[:, 4 + at % A_RING, :], scalar=cols[:, col:col + 1],
                    in1=parts[:, 3 * (kind == "K"), token_slice(b, c, tg)],
                    op0=ALU.add, op1=ALU.subtract).then_inc(rest_ready, 1)

            def tile_max(tile, j, qc):
                dve.wait_ge(smax_psum, tile + 1)
                at = 2 * (qc % 2)
                nc.vector.reduce_max(row_max[:, j % 2, qc:qc + 1],
                                     psum[:, at:at + 2, :].rearrange("p a q -> p (a q)"), AX_X).then_inc(smax_read, 1)

            def negate(head, j):
                dve.wait_ge(smax_read, (head + 1) * TB)
                nc.vector.tensor_scalar(neg_max[:, j % 2, 0, :], row_max[:, j % 2, :], -1.0, None,
                                        ALU.mult).then_inc(neg_high, 1)
                dve.wait_ge(neg_high, head + 1)
                nc.vector.scalar_tensor_tensor(out=neg_max[:, j % 2, 1, :], in0=row_max[:, j % 2, :], scalar=-1.0,
                                               in1=neg_max[:, j % 2, 0, :], op0=ALU.mult,
                                               op1=ALU.subtract).then_inc(neg_ready, 1)

            def first_maxima(tile):
                head, qc = divmod(tile, TB)
                tile_max(tile, head % HG, qc)
                if qc == TB - 1:
                    negate(head, head % HG)

            for i, (kind, b, tg, c) in enumerate(a_jobs):
                for tile in early_tiles(i):
                    if tile == 0:
                        modulation(1)
                    first_maxima(tile)
                if kind in "QK" and b == 0:
                    rest_part(qk_jobs.index(a_jobs[i]))
            for tile in range(early_tiles(len(a_jobs) - 1).stop, (HG + 1) * TB):
                first_maxima(tile)

            def residual(tg):
                for pair in range(2):
                    dve.wait_ge(c_psum, c_index["O", tg, pair] + 1)
                    t = 4 * tg + 2 * pair
                    dve.wait_ge(bo_added, t + 2)
                    nc.vector.tensor_tensor(x_sb[:, t:t + 2, :], psum[:, c_bank("O", tg, pair), :].rearrange("p (t d) -> p t d", d=D),
                                            x_sb[:, t:t + 2, :], ALU.add).then_inc(x1_ready, 1)
                dve.wait_ge(x1_ready, 2 * tg + 2)
                for t in range(4 * tg, 4 * tg + 4):
                    nc.vector.bn_stats(bn[:, t, :], x_sb[:, t, :]).then_inc(stats2_step, 1)
                dve.wait_ge(stats2_step, 4 * tg + 4)
                for t in range(4 * tg, 4 * tg + 4):
                    last = nc.vector.bn_aggr(mean_var[:, t, :], bn[:, t, :])
                last.then_inc(var2_ready, 1)

            def normalise2(b):
                dve.wait_ge(std2_ready, b + 1)
                nc.vector.reciprocal(rstd[:, b * TB:(b + 1) * TB], std[:, b * TB:(b + 1) * TB]).then_inc(rstd2_ready, 1)
                dve.wait_ge(rstd2_ready, b + 1)
                for tg in range(2 * b, 2 * b + 2):
                    if tg >= 2:
                        dve.wait_ge(c_psum, c_index["T", tg - 2, DC - 1] + 1)
                    for t in range(4):
                        at = 4 * tg + t
                        nc.vector.tensor_scalar(xhat2[:, tg % 2, t, :], x_sb[:, at, :], mean_var[:, at, 0:1],
                                                rstd[:, at:at + 1], ALU.subtract, ALU.mult).then_inc(xhat2_ready, 1)

            def split_xn2(tg, c, buffer):
                n, tokens = DC * tg + c, slice(tg * 512, (tg + 1) * 512)
                dve.wait_ge(xn2_full_ready, n + 1)
                nc.vector.tensor_copy(xn2_high[:, c, tokens], rest[:, buffer, :]).then_inc(xn2_high_ready, 1)
                dve.wait_ge(xn2_high_ready, n + 1)
                nc.vector.tensor_tensor(xn2_low[:, c, tokens], rest[:, buffer, :], xn2_high[:, c, tokens],
                                        ALU.subtract).then_inc(xn2_ready, 1)

            def early_c_job(kind, tg, c):
                if kind == "O":
                    if c == 1:
                        residual(tg)
                    if c == 1 and tg == 1:
                        normalise2(0)
                    return
                dve.wait_ge(c_psum, c_index[kind, tg, c] + 1)
                src = psum[:, c_bank(kind, tg, c), :]
                if kind == "A":
                    nc.vector.tensor_copy(attn_t[:, tg % 2, c, :], src).then_inc(attn_t_ready, 1)
                else:
                    if DC * tg + c:
                        dve.wait_ge(xn2_ready, DC * tg + c)
                    nc.vector.tensor_scalar(rest[:, 1, :], src, mod_mul[:, 1, c, 0:1], mod_add[:, 1, c, 0:1],
                                            ALU.mult, ALU.add).then_inc(xn2_full_ready, 1)
                    split_xn2(tg, c, 1)

            for group in range(NG):
                for step in range(STEPS):
                    ahead = (group + 1) * HG + 1 + step // 4
                    qc = (2 * step) % TB
                    if ahead < NG * HG:
                        tile_max(ahead * TB + qc, ahead % HG, qc)
                        tile_max(ahead * TB + qc + 1, ahead % HG, qc + 1)
                        if step % 4 == 3:
                            negate(ahead, ahead % HG)
                    if step % TB == TB - 1:
                        half = step // TB
                        dve.wait_ge(misc_psum, misc_use(group + 1, 2 * half + 1) + 1 if group + 1 < NG
                                    else misc_use(NG, half))
                        sums = psum[:, MISC_BANK, :].rearrange("p (t j w) -> p t j w", t=4, j=HG)
                        rs = rsum[:, :].rearrange("p (t j) -> p t j", t=4)
                        nc.vector.reciprocal(rs, sums[:, :, :, HD]).then_inc(rsum_ready, 1)
                        dve.wait_ge(rsum_ready, group * 2 + half + 1)
                        dst = attn_out[:, group // 2, 4 * half:4 * half + 4, group % 2, :].rearrange(
                            "p t (j d) -> p t j d", j=HG)
                        nc.vector.tensor_tensor(dst, sums[:, :, :, 0:HD],
                                                rs.unsqueeze(3).broadcast_to([P, 4, HG, HD]),
                                                ALU.mult).then_inc(attn_ready, 1)
                    if group + 1 == NG:
                        for job in c_early.get(step, ()):
                            early_c_job(*job)

            def add_output(tg):
                for pair in range(2):
                    dve.wait_ge(out_psum, tg * 2 + (pair + 1))
                    rows_of = x_sb[:, bass.ds(tg * 4 + 2 * pair, 2), :]
                    nc.vector.tensor_tensor(rows_of, psum[:, 6 + pair, :].rearrange("p (t d) -> p t d", d=D),
                                            rows_of, ALU.add).then_inc(out_ready, 1)

            def split_hidden(tg, last_output=False, chunks=range(FC)):
                for f in chunks:
                    dve.wait_ge(hid_full_ready, tg * FC + (f + 1))
                    nc.vector.tensor_copy(hid_high[:, f, :], hid_full[:, f % HID_RING, :]).then_inc(hid_high_ready, 1)
                    dve.wait_ge(hid_high_ready, tg * FC + (f + 1))
                    nc.vector.tensor_tensor(hid_low[:, f, :], hid_full[:, f % HID_RING, :], hid_high[:, f, :],
                                            ALU.subtract).then_inc(hid_ready, 1)
                    if f == 3 and last_output:
                        add_output(tg - 1)

            split_hidden(0, chunks=range(0, 3))
            residual(2)
            split_hidden(0, chunks=range(3, 4))
            residual(3)
            normalise2(1)
            split_hidden(0, chunks=range(4, FC))
            for kind, tg, c in c_late:
                split_xn2(tg, c, c)
            with dve.Fori(1, TG) as tg:
                split_hidden(tg, last_output=True)
            add_output(TG - 1)


_INS = ["x", "cond_1024"] + ["L0_cond_" + n for n in (
    "ln1_w", "ln1_b", "ln2_w", "ln2_b", "wq", "bq", "wk", "bk", "wv", "bv", "wo", "bo",
    "wt_attn", "bt_attn", "wt_ffn", "bt_ffn", "w1", "b1", "w2", "b2")]


def kernel(**inputs):
    import numpy as np
    import concourse.bacc as bacc
    from concourse.bass_utils import run_bass_kernel_spmd

    nc = bacc.Bacc("TRN2", target_bir_lowering=False, num_devices=1)
    arrays, args = {}, []
    for name in _INS:
        a = np.ascontiguousarray(inputs[name])
        arrays["in_" + name] = a
        args.append(nc.dram_tensor("in_" + name, a.shape, mybir.dt.from_np(a.dtype), kind="ExternalInput").ap())
    args.append(nc.dram_tensor("out_dram", arrays["in_x"].shape, F32, kind="ExternalOutput").ap())
    layer_program(nc, *args)
    r = run_bass_kernel_spmd(nc, [arrays], core_ids=[0])
    return r.results[0]["out_dram"]
```
